# Optimizing a Trainium2 kernel written in Bass

```python
import numpy as np
import jax
import jax.numpy as jnp

def _softmax(x, axis=-1):
    return jax.nn.softmax(x, axis=axis)

def _gelu(x):
    return jax.nn.gelu(x, approximate=True)

def _silu(x):
    return jax.nn.silu(x)

def _sigmoid(x):
    return jax.nn.sigmoid(x)

def _layernorm(x, axis=-1, eps=1e-05):
    m = jnp.mean(x, axis=axis, keepdims=True)
    v = jnp.var(x, axis=axis, keepdims=True)
    return (x - m) / jnp.sqrt(v + eps)

def _scatter_add(tgt, idx, src, axis=0):
    return tgt.at[idx].add(src)

def _segment_sum(src, seg, n):
    return jax.ops.segment_sum(src, seg, n)
kernel_name = 'mk_adj_resnorm_d1_adj_r2_6009de'

def setup_inputs(seed: int=0):
    np.random.seed(seed)
    _w = jnp.asarray

    def _rec_inputs():
        import jax
        import jax.numpy as jnp
        _gk = jax.random.key(seed)
        x = -0.0005207 + 1.001 * jax.random.normal(jax.random.fold_in(_gk, 1), (3327, 128), jnp.float32)
        _a = jax.random.bernoulli(jax.random.fold_in(_gk, 2), 0.00240457, (3327, 3327))
        _a = jnp.logical_or(_a, jnp.eye(3327, dtype=bool))
        _af = _a.astype(jnp.float32)
        _af = _af * jax.random.uniform(jax.random.fold_in(_gk, 3), (3327, 3327), jnp.float32, 0.05, 1)
        adj = _af
        return (x, adj)
    x, adj = _rec_inputs()

    def _L0_gnn_setup():
        import jax, jax.numpy as jnp
        import numpy as np
        D_IN = 128
        D_ATTN = 64
        STEPS = 2
        TOP_P = 0.9
        TAU = 1.0
        LN_EPS = 1e-05
        N_NODES = 4096

        def _top_p_attention(X, W1, W2, W3):
            q = X @ W1.T @ W2.T
            k = X @ W3.T
            logits = q @ k.T / TAU
            probs = jax.nn.softmax(logits, axis=-1)
            idx = jnp.argsort(-probs, axis=-1)
            sp = jnp.take_along_axis(probs, idx, axis=-1)
            cs = jnp.cumsum(sp, axis=-1)
            keep_sorted = cs - sp < TOP_P
            rows = jnp.arange(probs.shape[0])[:, None]
            mask = jnp.zeros(probs.shape, dtype=bool).at[rows, idx].set(keep_sorted)
            A = probs * mask
            return A / jnp.maximum(A.sum(-1, keepdims=True), 1e-12)
        key = jax.random.key(seed)
        ks = jax.random.split(key, 8)
        N, d, da, steps = (N_NODES, D_IN, D_ATTN, STEPS)
        X = jax.random.normal(ks[0], (N, d), dtype=jnp.float32)
        S = jax.random.uniform(ks[1], (N, N), dtype=jnp.float32)
        W1 = jax.random.normal(ks[2], (da, d), dtype=jnp.float32) / np.sqrt(d)
        W2 = jax.random.normal(ks[3], (da, da), dtype=jnp.float32) / np.sqrt(da)
        W3 = jax.random.normal(ks[4], (da, d), dtype=jnp.float32) / np.sqrt(d)
        U1 = jax.random.normal(ks[5], (steps, d, d), dtype=jnp.float32) / np.sqrt(d)
        U2 = jax.random.normal(ks[6], (steps, d, d), dtype=jnp.float32) / np.sqrt(d)
        ln_g = jnp.ones((d,), dtype=jnp.float32)
        ln_b = jnp.zeros((d,), dtype=jnp.float32)
        return {'X': X, 'S': S, 'W1': W1, 'W2': W2, 'W3': W3, 'U1': U1, 'U2': U2, 'ln_g': ln_g, 'ln_b': ln_b}
    _L0_gnn_all = _L0_gnn_setup()
    _L0_gnn_in = {k: v for k, v in _L0_gnn_all.items() if k in ('W1', 'W2', 'W3', 'U1', 'U2', 'ln_g', 'ln_b')}
    del _L0_gnn_all
    return {'x': x, 'adj': adj, 'L0_gnn_W1': _L0_gnn_in['W1'], 'L0_gnn_W2': _L0_gnn_in['W2'], 'L0_gnn_W3': _L0_gnn_in['W3'], 'L0_gnn_U1': _L0_gnn_in['U1'], 'L0_gnn_U2': _L0_gnn_in['U2'], 'L0_gnn_ln_g': _L0_gnn_in['ln_g'], 'L0_gnn_ln_b': _L0_gnn_in['ln_b']}

def reference(x, adj, L0_gnn_W1, L0_gnn_W2, L0_gnn_W3, L0_gnn_U1, L0_gnn_U2, L0_gnn_ln_g, L0_gnn_ln_b):
    import jax
    import jax.numpy as jnp

    def _L0_gnn_ref(X, S, W1, W2, W3, U1, U2, ln_g, ln_b):
        import jax, jax.numpy as jnp
        import numpy as np
        D_IN = 128
        D_ATTN = 64
        STEPS = 2
        TOP_P = 0.9
        TAU = 1.0
        LN_EPS = 1e-05
        N_NODES = 4096

        def _top_p_attention(X, W1, W2, W3):
            q = X @ W1.T @ W2.T
            k = X @ W3.T
            logits = q @ k.T / TAU
            probs = jax.nn.softmax(logits, axis=-1)
            idx = jnp.argsort(-probs, axis=-1)
            sp = jnp.take_along_axis(probs, idx, axis=-1)
            cs = jnp.cumsum(sp, axis=-1)
            keep_sorted = cs - sp < TOP_P
            rows = jnp.arange(probs.shape[0])[:, None]
            mask = jnp.zeros(probs.shape, dtype=bool).at[rows, idx].set(keep_sorted)
            A = probs * mask
            return A / jnp.maximum(A.sum(-1, keepdims=True), 1e-12)
        N = X.shape[0]
        R = S + jnp.eye(N, dtype=X.dtype)
        R = R / R.sum(-1, keepdims=True)
        Z = jnp.zeros_like(X)
        Xf = X
        Xa = X
        for n in range(STEPS):
            A = _top_p_attention(Xa, W1, W2, W3)
            Xf = R @ Xf
            Xa = A @ Xa
            Z = Z + Xf @ U1[n].T + Xa @ U2[n].T
        h = X + Z
        mu = h.mean(-1, keepdims=True)
        var = jnp.mean((h - mu) ** 2, axis=-1, keepdims=True)
        return (h - mu) / jnp.sqrt(var + LN_EPS) * ln_g + ln_b
    x = _layernorm(x + _L0_gnn_ref(x, adj, L0_gnn_W1, L0_gnn_W2, L0_gnn_W3, L0_gnn_U1, L0_gnn_U2, L0_gnn_ln_g, L0_gnn_ln_b), axis=-1)
    return x

_drawn_inputs = setup_inputs


def setup_inputs(seed=0):
    import zlib

    import numpy as np

    out = dict(_drawn_inputs(seed))
    spreads = {'L0_gnn_ln_g': (1.0, 0.2), 'L0_gnn_ln_b': (0.0, 0.1)}
    factors = {}
    for name, (base, spread) in spreads.items():
        noise = np.random.default_rng([zlib.crc32(name.encode()), seed]).standard_normal(out[name].shape)
        drawn = base * np.exp(spread * noise) if base else spread * noise
        out[name] = jnp.asarray(drawn.astype(out[name].dtype))
    for name, factor in factors.items():
        out[name] = (out[name] * factor).astype(out[name].dtype)
    return out
```

```python
import concourse.bass as bass
from concourse import mybir
from contextlib import ExitStack
import numpy as np


def gnn_top_p_kernel(nc, x, adj, W1, W2, W3, U1, U2, ln_g, ln_b, out):
    fp32 = mybir.dt.float32
    bf16 = mybir.dt.bfloat16
    ALU = mybir.AluOpType
    ACT = mybir.ActivationFunctionType
    AX = mybir.AxisListType

    P = 128
    N, D = x.shape
    DA = W1.shape[0]
    STEPS = U1.shape[0]
    NT = (N + P - 1) // P
    LAST = N - (NT - 1) * P
    NP = NT * P
    BANK = 512
    CH = BANK // P
    NCH = (NT + CH - 1) // CH
    CW = [min(BANK, NP - c * BANK) for c in range(NCH)]
    LW = [min(BANK, N - c * BANK) for c in range(NCH)]
    LN_EPS = 1e-5
    DROP = float(np.float32(1.0) - np.float32(0.9))
    LOG_RANGE = float(np.log(NP / DROP) + 0.1)
    K = 24
    FACT = [float(np.exp(LOG_RANGE / 2 ** (k + 1))) for k in range(K)]
    BIG = 1e30
    assert NT % 2 == 0

    ctx = ExitStack()
    with ctx:
        def sb(name, shape, dt=fp32):
            return ctx.enter_context(nc.sbuf_tensor(name, shape, dt))

        def pb(name):
            return ctx.enter_context(nc.psum_tensor(name, [P, BANK], fp32))

        def sem(name):
            return ctx.enter_context(nc.semaphore(name))

        X0 = sb("X0", [P, NT, D + 1])
        XF = sb("XF", [P, NT, D + 1])
        XA = sb("XA", [P, NT, D])
        H = sb("H", [P, NT, D])
        ident = sb("ident", [P, P])
        u_in = sb("u_in", [P, 2 * STEPS, D])
        w_in = sb("w_in", [DA, 2, D])
        w2_in = sb("w2_in", [DA, DA])
        UT = sb("UT", [P, 2 * STEPS, D])
        WT = sb("WT", [P, 2, DA])
        W2T = sb("W2T", [DA, DA])
        gb = sb("gb", [P, 2, D])
        xT = sb("xT", [P, 2, BANK])
        x1T = sb("x1T", [DA, BANK])
        kT = sb("kT", [DA, NP])
        qT = sb("qT", [DA, NP])
        q_tile = sb("q_tile", [DA, 2, P])
        E = sb("E", [P, 2, NP])
        junk = sb("junk", [P, NP])
        eq = sb("eq", [P, NP], bf16)
        A = sb("A", [P, NP])
        S = sb("S", [P, 2, NP])
        blkT = sb("blkT", [P, 2, BANK])
        newF = sb("newF", [P, D])
        newA = sb("newA", [P, D])
        newT = sb("newT", [P, 2, P])
        top8 = sb("top8", [P, 8])
        negm = sb("negm", [P, 2])
        Z = sb("Z", [P, 2])
        st = sb("st", [P, 16])
        w8 = sb("w8", [P, 8])
        c8 = sb("c8", [P, 8])
        d8 = sb("d8", [P, 8])
        ones8 = sb("ones8", [P, 8])
        fin = sb("fin", [P, 4])
        den = sb("den", [P, 2])
        mv = sb("mv", [P, NT])
        sd = sb("sd", [P, NT])
        rs = sb("rs", [P, NT])

        logit_ps = [pb("logit_ps0"), pb("logit_ps1")]
        blk_ps = [pb("blk_ps0"), pb("blk_ps1")]
        racc = pb("racc")
        aacc = pb("aacc")
        newT_ps = pb("newT_ps")
        h_ps = pb("h_ps")

        x_loaded = sem("x_loaded")
        w_loaded = sem("w_loaded")
        adj_loaded = [sem("adj_loaded0"), sem("adj_loaded1")]
        pad_zeroed = sem("pad_zeroed")
        pool_step = sem("pool_step")
        setup_done = sem("setup_done")
        wT_ready = sem("wT_ready")
        wT_done = sem("wT_done")
        xT_ready = sem("xT_ready")
        xT_done = sem("xT_done")
        k_ready = sem("k_ready")
        k_done = sem("k_done")
        x1_ready = sem("x1_ready")
        x1_done = sem("x1_done")
        q_ready = sem("q_ready")
        q_done = sem("q_done")
        qt_ready = sem("qt_ready")
        logits_ready = sem("logits_ready")
        logits_done = sem("logits_done")
        max_ready = sem("max_ready")
        e_ready = sem("e_ready")
        a_ready = sem("a_ready")
        blk_ready = sem("blk_ready")
        blk_done = sem("blk_done")
        blk_used = sem("blk_used")
        new_ready = sem("new_ready")
        new_saved = sem("new_saved")
        newT_ready = sem("newT_ready")
        newT_done = sem("newT_done")
        h_ready = sem("h_ready")
        h_done = sem("h_done")
        s_search = sem("s_search")
        s_new = sem("s_new")
        s_max = sem("s_max")
        s_fin = sem("s_fin")
        var_ready = sem("var_ready")
        sd_ready = sem("sd_ready")
        out_ready = sem("out_ready")
        out_written = sem("out_written")

        block = ctx.enter_context(nc.Block())

        def over_tiles(eng, s, body):
            body(0, s * NT, 0, True, False)
            with eng.Fori(0, (NT - 2) // 2) as p:
                for j in (1, 2):
                    body(2 * p + j, 2 * p + (s * NT + j), j % 2, False, False)
            body(NT - 1, s * NT + NT - 1, (NT - 1) % 2, False, True)

        @block.sync
        def _(sp):
            sp.dma_start(X0[:, 0:NT - 1, 0:D], x[0:(NT - 1) * P, :].rearrange("(t p) d -> p t d", p=P)).then_inc(x_loaded, 16)
            sp.wait_ge(pad_zeroed, 1)
            sp.dma_start(X0[0:LAST, NT - 1, 0:D], x[(NT - 1) * P:N, :]).then_inc(x_loaded, 16)
            for n in range(STEPS):
                sp.dma_start(u_in[:, n, :], U1[n, :, :]).then_inc(w_loaded, 16)
                sp.dma_start(u_in[:, STEPS + n, :], U2[n, :, :]).then_inc(w_loaded, 16)
            sp.dma_start(w_in[:, 0, :], W1[:, :]).then_inc(w_loaded, 16)
            sp.dma_start(w_in[:, 1, :], W3[:, :]).then_inc(w_loaded, 16)
            sp.dma_start(w2_in[:, :], W2[:, :]).then_inc(w_loaded, 16)
            for n, v in enumerate((ln_g, ln_b)):
                sp.dma_start(gb[:, n, :], v.rearrange("(a d) -> a d", a=1).to_broadcast([P, D])).then_inc(w_loaded, 16)
            for s in range(STEPS):
                def load_pair(p, short):
                    for j in range(2):
                        g = 2 * p + (s * NT + j)
                        if not (s == 0 and isinstance(p, int) and p == 0):
                            sp.wait_ge(blk_ready, (g - 2) * (2 * NCH) + NCH)
                        r0 = (2 * p + j) * P
                        if short and j == 1:
                            m = LAST // 16 * 16
                            sp.dma_start(S[0:m, j, 0:N], adj[r0:r0 + m, :]).then_inc(adj_loaded[j], 16)
                            sp.dma_start(S[m:LAST, j, 0:N], adj[r0 + m:N, :]).then_inc(adj_loaded[j], 16)
                        else:
                            sp.dma_start(S[:, j, 0:N], adj[bass.ds(r0, P), :]).then_inc(adj_loaded[j], 16)
                load_pair(0, False)
                with sp.Fori(1, NT // 2 - 1) as p:
                    load_pair(p, False)
                load_pair(NT // 2 - 1, True)
            sp.wait_ge(out_ready, 1)
            sp.dma_start(out[0:(NT - 1) * P, :].rearrange("(t p) d -> p t d", p=P), H[:, 0:NT - 1, :]).then_inc(out_written, 16)
            sp.dma_start(out[(NT - 1) * P:N, :], H[0:LAST, NT - 1, :]).then_inc(out_written, 16)
            sp.wait_ge(out_written, 32)

        @block.gpsimd
        def _(pool):
            pool.memset(ident[:, :], 0.0).then_inc(pool_step, 1)
            pool.wait_ge(pool_step, 1)
            pool.affine_select(out=ident[:, :], in_=ident[:, :], compare_op=ALU.not_equal, fill=1.0,
                               base=0, pattern=[[-1, P]], channel_multiplier=1).then_inc(setup_done, 1)
            pool.memset(X0[:, :, D:D + 1], 1.0).then_inc(setup_done, 1)
            pool.memset(XF[:, :, D:D + 1], 1.0).then_inc(setup_done, 1)
            pool.memset(S[:, :, N:NP], 0.0).then_inc(setup_done, 1)
            pool.memset(E[:, :, N:NP], 0.0).then_inc(setup_done, 1)
            pool.memset(ones8[:, :], 1.0).then_inc(setup_done, 1)

            for s in range(STEPS):
                def fetch_q(t, g, par):
                    if s or not isinstance(t, int) or t >= 2:
                        pool.wait_ge(logits_ready, (g - 1) * NCH)
                    pool.tensor_copy(q_tile[:, par, :], qT[:, bass.ds(t * P, P)]).then_inc(qt_ready, 1)

                def save_new(t, g):
                    if s == 0:
                        pool.wait_ge(new_ready, g + 1)
                        pool.tensor_copy(XF[:, bass.ds(t, 1), 0:D], newF[:, :].rearrange("p (a d) -> p a d", a=1))
                        pool.tensor_copy(XA[:, bass.ds(t, 1), :], newA[:, :].rearrange("p (a d) -> p a d", a=1)).then_inc(new_saved, 1)

                pool.wait_ge(q_done, (s + 1) * NCH)
                fetch_q(0, s * NT, 0)

                def body(t, g, par, first, last):
                    if not last:
                        fetch_q(t + 1, g + 1, 1 - par)
                    if not first:
                        save_new(t - 1, g - 1)
                over_tiles(pool, s, body)
                save_new(NT - 1, s * NT + NT - 1)

        @block.tensor
        def _(pe):
            pe.wait_ge(setup_done, 1)
            pe.wait_ge(w_loaded, 16 * (2 * STEPS + 5))
            for n in range(2 * STEPS):
                pe.transpose(blk_ps[0][:, n * P:(n + 1) * P], u_in[:, n, :], ident[:, :])
            for n in range(2):
                pe.transpose(blk_ps[1][:, n * DA:(n + 1) * DA], w_in[:, n, :], ident[0:DA, 0:DA])
            pe.transpose(blk_ps[1][0:DA, 2 * DA:3 * DA], w2_in[:, :], ident[0:DA, 0:DA]).then_inc(wT_ready, 1)
            pe.wait_ge(wT_done, 3)
            pe.wait_ge(x_loaded, 32)

            for s in range(STEPS):
                Xf, Xa = (X0, X0) if s == 0 else (XF, XA)
                if s:
                    pe.wait_ge(new_saved, s * NT)
                for c in range(NCH):
                    n = s * NCH + c
                    w = CW[c]
                    if n >= 2:
                        pe.wait_ge(xT_done, n - 1)
                    for b in range(w // P):
                        last = pe.transpose(blk_ps[c % 2][:, b * P:(b + 1) * P], Xa[:, c * CH + b, 0:D], ident[:, :])
                    last.then_inc(xT_ready, 1)
                    pe.wait_ge(xT_done, n + 1)
                    if n:
                        pe.wait_ge(k_done, n)
                    pe.matmul(racc[0:DA, 0:w], WT[:, 1, :], xT[:, c % 2, 0:w], start=True, stop=True).then_inc(k_ready, 1)
                    if n:
                        pe.wait_ge(x1_done, n)
                    pe.matmul(aacc[0:DA, 0:w], WT[:, 0, :], xT[:, c % 2, 0:w], start=True, stop=True).then_inc(x1_ready, 1)
                    pe.wait_ge(x1_done, n + 1)
                    if n:
                        pe.wait_ge(q_done, n)
                    pe.matmul(newT_ps[0:DA, 0:w], W2T[:, :], x1T[:, 0:w], start=True, stop=True).then_inc(q_ready, 1)
                pe.wait_ge(k_done, (s + 1) * NCH)
                pe.wait_ge(q_done, (s + 1) * NCH)

                def logits(g, par):
                    pe.wait_ge(qt_ready, g + 1)
                    for c in range(NCH):
                        if not (isinstance(g, int) and g == 0 and c < 2):
                            pe.wait_ge(logits_done, g * NCH + (c - 1))
                        pe.matmul(logit_ps[(c + par) % 2][:, 0:LW[c]], q_tile[:, par, :],
                                  kT[:, c * BANK:c * BANK + LW[c]], start=True, stop=True).then_inc(logits_ready, 1)

                def product(src, rhs, width, acc, base, odd):
                    def turn(c):
                        if not (isinstance(base, int) and base + c < 2):
                            pe.wait_ge(blk_done, base + (c - 1))
                        for b in range(CW[c] // P):
                            j = c * CH + b
                            m = pe.transpose(blk_ps[(c + odd) % 2][:, b * P:(b + 1) * P], src[:, j * P:(j + 1) * P], ident[:, :])
                        m.then_inc(blk_ready, 1)
                    turn(0)
                    for c in range(NCH):
                        if c + 1 < NCH:
                            turn(c + 1)
                        pe.wait_ge(blk_done, base + (c + 1))
                        for b in range(CW[c] // P):
                            j = c * CH + b
                            m = pe.matmul(acc[:, 0:width], blkT[:, (c + odd) % 2, b * P:(b + 1) * P], rhs[:, j, 0:width],
                                          start=(j == 0), stop=(j == NT - 1))
                        m.then_inc(blk_used, 1)

                def tile_out(g):
                    pe.wait_ge(new_ready, g + 1)
                    if not (isinstance(g, int) and g == 0):
                        pe.wait_ge(newT_done, g)
                    pe.transpose(newT_ps[:, 0:P], newF[:, :], ident[:, :])
                    pe.transpose(newT_ps[:, P:2 * P], newA[:, :], ident[:, :]).then_inc(newT_ready, 1)
                    pe.wait_ge(newT_done, g + 1)
                    if not (isinstance(g, int) and g == 0):
                        pe.wait_ge(h_done, g)
                    pe.matmul(h_ps[:, 0:D], newT[:, 0, :], UT[:, s, :], start=True, stop=False)
                    pe.matmul(h_ps[:, 0:D], newT[:, 1, :], UT[:, STEPS + s, :], start=False, stop=True).then_inc(h_ready, 1)

                logits(s * NT, 0)

                def body(t, g, par, first, last):
                    if not last:
                        logits(g + 1, 1 - par)
                    pe.wait_ge(adj_loaded[par], 8 * g + (8 * (2 - par) + (16 * s if par else 0) + (16 if last else 0)))
                    if not (isinstance(g, int) and g == 0):
                        pe.wait_ge(new_ready, g)
                    product(S[:, par, :], Xf, D + 1, racc, g * (2 * NCH), 0)
                    if not first:
                        tile_out(g - 1)
                    pe.wait_ge(a_ready, g + 1)
                    product(A, Xa, D, aacc, g * (2 * NCH) + NCH, NCH % 2)
                over_tiles(pe, s, body)
                tile_out(s * NT + NT - 1)

        @block.scalar
        def _(act):
            act.wait_ge(wT_ready, 1)
            act.activation(UT[:, :, :], blk_ps[0][:, :].rearrange("p (n d) -> p n d", n=2 * STEPS), ACT.Copy).then_inc(wT_done, 1)
            act.activation(WT[:, :, :], blk_ps[1][:, 0:2 * DA].rearrange("p (n d) -> p n d", n=2), ACT.Copy).then_inc(wT_done, 1)
            act.activation(W2T[:, :], blk_ps[1][0:DA, 2 * DA:3 * DA], ACT.Copy).then_inc(wT_done, 1)
            act.wait_ge(setup_done, 6)
            for s in range(STEPS):
                for c in range(NCH):
                    n = s * NCH + c
                    act.wait_ge(xT_ready, n + 1)
                    if n >= 2:
                        act.wait_ge(x1_ready, n - 1)
                    act.activation(xT[:, c % 2, 0:CW[c]], blk_ps[c % 2][:, 0:CW[c]], ACT.Copy).then_inc(xT_done, 1)
                    act.wait_ge(x1_ready, n + 1)
                    if n:
                        act.wait_ge(q_ready, n)
                    act.activation(x1T[:, 0:CW[c]], aacc[0:DA, 0:CW[c]], ACT.Copy).then_inc(x1_done, 1)

                def store_logits(g, par):
                    if not (isinstance(g, int) and g < 2):
                        act.wait_ge(a_ready, g - 1)
                    for c in range(NCH):
                        act.wait_ge(logits_ready, g * NCH + (c + 1))
                        act.activation(E[:, par, c * BANK:c * BANK + LW[c]], logit_ps[(c + par) % 2][:, 0:LW[c]],
                                       ACT.Copy).then_inc(logits_done, 1)

                def exponentials(g, par):
                    act.wait_ge(max_ready, g + 1)
                    act.activation(E[:, par, 0:N], E[:, par, 0:N], ACT.Exp, bias=negm[:, par:par + 1], scale=1.0,
                                   accum_out=Z[:, par:par + 1]).then_inc(e_ready, 1)

                def empty_blocks(base, odd):
                    for c in range(NCH):
                        act.wait_ge(blk_ready, base + (c + 1))
                        if not (isinstance(base, int) and base + c < 2):
                            act.wait_ge(blk_used, base + (c - 1))
                        act.activation(blkT[:, (c + odd) % 2, 0:CW[c]], blk_ps[(c + odd) % 2][:, 0:CW[c]],
                                       ACT.Copy).then_inc(blk_done, 1)

                def empty_new(g):
                    act.wait_ge(newT_ready, g + 1)
                    if not (isinstance(g, int) and g == 0):
                        act.wait_ge(h_ready, g)
                    act.activation(newT[:, :, :], newT_ps[:, 0:2 * P].rearrange("p (n d) -> p n d", n=2),
                                   ACT.Copy).then_inc(newT_done, 1)

                store_logits(s * NT, 0)
                exponentials(s * NT, 0)

                def body(t, g, par, first, last):
                    if not last:
                        store_logits(g + 1, 1 - par)
                    empty_blocks(g * (2 * NCH), 0)
                    if not first:
                        empty_new(g - 1)
                    if not last:
                        exponentials(g + 1, 1 - par)
                    empty_blocks(g * (2 * NCH) + NCH, NCH % 2)
                over_tiles(act, s, body)
                empty_new(s * NT + NT - 1)
            for n in range(2):
                act.wait_ge(var_ready, n + 1)
                act.activation(sd[:, :], sd[:, :], ACT.Sqrt).then_inc(sd_ready, 1)

        @block.vector
        def _(dve):
            v = nc.vector
            v.memset(X0[96:P, NT - 1, 0:D], 0.0).then_inc(pad_zeroed, 1)

            class Chain:
                def __init__(self, sem, base):
                    self.sem, self.base, self.n = sem, base, 0

                def post(self, ins):
                    self.n += 1
                    ins.then_inc(self.sem, 1)

                def __call__(self, ins):
                    self.post(ins)
                    dve.wait_ge(self.sem, self.base + self.n)

            def col(n, m=1):
                return st[:, n:n + m]

            DROPZ, THR, LOW, PICK, LOWHI, ROOM, TSTAR, SGT, TIES, KEPT, MASS, FLOOR = range(12)
            N_SEARCH = 4 * K + 22

            for s in range(STEPS):
                Xf = X0 if s == 0 else XF
                for c in range(NCH):
                    n = s * NCH + c
                    dve.wait_ge(k_ready, n + 1)
                    v.tensor_copy(kT[:, c * BANK:c * BANK + CW[c]], racc[0:DA, 0:CW[c]]).then_inc(k_done, 1)
                    dve.wait_ge(q_ready, n + 1)
                    v.tensor_copy(qT[:, c * BANK:c * BANK + CW[c]], newT_ps[0:DA, 0:CW[c]]).then_inc(q_done, 1)

                def row_max(g, par):
                    dve.wait_ge(logits_done, (g + 1) * NCH)
                    v.reduce_max(fin[:, 2:3], E[:, par, 0:N], AX.X).then_inc(s_max, 1)
                    dve.wait_ge(s_max, g + 1)
                    v.tensor_scalar(negm[:, par:par + 1], fin[:, 2:3], -1.0, None, ALU.mult).then_inc(max_ready, 1)

                def descend(link, e, ks):
                    for k in ks:
                        nxt = FACT[k + 1] if k + 1 < K else 1.0
                        link(v.scalar_tensor_tensor(out=junk[:, :], in0=e, scalar=col(THR), in1=e, op0=ALU.is_lt,
                                                    op1=ALU.mult, accum_out=col(LOW)))
                        link(v.tensor_scalar(col(PICK), col(LOW), col(DROPZ), None, ALU.is_le))
                        link(v.tensor_scalar(col(PICK), col(PICK), nxt - nxt / FACT[k], nxt / FACT[k], ALU.mult, ALU.add))
                        link(v.tensor_tensor(col(THR), col(THR), col(PICK), ALU.mult))

                def search_begin(link, e, g, par):
                    dve.wait_ge(e_ready, g + 1)
                    link(v.tensor_scalar(col(DROPZ), Z[:, par:par + 1], DROP, None, ALU.mult))
                    link(v.tensor_scalar(col(THR), col(DROPZ), FACT[0] / NP, None, ALU.mult))

                def search_end(link, e, g, par):
                    link(v.tensor_scalar(col(THR), col(THR), FACT[K - 1] * (1.0 + 2e-6), None, ALU.mult))
                    link(v.scalar_tensor_tensor(out=junk[:, :], in0=e, scalar=col(THR), in1=e, op0=ALU.is_lt,
                                                op1=ALU.mult, accum_out=col(LOWHI)))
                    link.post(v.tensor_tensor(col(ROOM), col(LOWHI), col(DROPZ), ALU.subtract))
                    link(v.max(w8[:, :], junk[:, :]))
                    link(v.tensor_tensor_scan(c8[:, :], ones8[:, :], w8[:, :], 0.0, ALU.mult, ALU.add))
                    link(v.tensor_tensor(d8[:, :], c8[:, :], w8[:, :], ALU.subtract))
                    link(v.tensor_scalar(d8[:, :], d8[:, :], col(ROOM), BIG, ALU.is_ge, ALU.mult))
                    link(v.tensor_tensor(d8[:, :], d8[:, :], w8[:, :], ALU.max))
                    link(v.tensor_reduce(col(TSTAR), d8[:, :], AX.X, ALU.min))
                    if not (isinstance(g, int) and g == 0):
                        dve.wait_ge(blk_ready, g * (2 * NCH))
                    link(v.scalar_tensor_tensor(out=A[:, :], in0=e, scalar=col(TSTAR), in1=e, op0=ALU.is_gt,
                                                op1=ALU.mult, accum_out=col(SGT)))
                    link(v.tensor_tensor(col(TIES), Z[:, par:par + 1], col(SGT), ALU.subtract))
                    link(v.reciprocal(col(MASS), col(TSTAR)))
                    link(v.scalar_tensor_tensor(out=col(TIES), in0=col(TIES), scalar=col(DROPZ), in1=col(MASS),
                                                op0=ALU.subtract, op1=ALU.mult))
                    link(v.tensor_scalar(col(TIES), col(TIES), 0.5, 1.0, ALU.max, ALU.add))
                    link(v.tensor_scalar(eq[:, :], e, col(TSTAR), None, ALU.is_equal))
                    link(v.tensor_tensor_scan(junk[:, :], eq[:, :], eq[:, :], 0.0, ALU.add, ALU.max))
                    link(v.scalar_tensor_tensor(out=eq[:, :], in0=junk[:, :], scalar=col(TIES), in1=eq[:, :],
                                                op0=ALU.is_lt, op1=ALU.mult, accum_out=col(KEPT)))
                    link(v.scalar_tensor_tensor(out=col(MASS), in0=col(KEPT), scalar=col(TSTAR), in1=col(SGT),
                                                op0=ALU.mult, op1=ALU.add))
                    link(v.scalar_tensor_tensor(out=col(MASS), in0=Z[:, par:par + 1], scalar=1e-12, in1=col(MASS),
                                                op0=ALU.mult, op1=ALU.max))
                    link(v.reciprocal(den[:, par:par + 1], col(MASS)))
                    v.scalar_tensor_tensor(out=A[:, :], in0=eq[:, :], scalar=col(TSTAR), in1=A[:, :],
                                           op0=ALU.mult, op1=ALU.add).then_inc(a_ready, 1)

                def new_features(t, g, par):
                    link = Chain(s_new, g * 4)
                    dve.wait_ge(blk_used, g * (2 * NCH) + NCH)
                    link(v.tensor_scalar(fin[:, 0:1], racc[:, D:D + 1], 1.0, None, ALU.add))
                    link(v.reciprocal(fin[:, 1:2], fin[:, 0:1]))
                    if not (isinstance(g, int) and g == 0):
                        dve.wait_ge(newT_ready, g)
                        if s == 0:
                            dve.wait_ge(new_saved, g)
                    link(v.tensor_tensor(newF[:, :], racc[:, 0:D], Xf[:, bass.ds(t, 1), 0:D].rearrange("p a d -> p (a d)"), ALU.add))
                    link(v.tensor_scalar(newF[:, :], newF[:, :], fin[:, 1:2], None, ALU.mult))
                    dve.wait_ge(blk_used, (g + 1) * (2 * NCH))
                    v.tensor_scalar(newA[:, :], aacc[:, 0:D], den[:, par:par + 1], None, ALU.mult).then_inc(new_ready, 1)

                def add_out(t, g):
                    dve.wait_ge(h_ready, g + 1)
                    base = X0 if s == 0 else H
                    v.tensor_tensor(H[:, bass.ds(t, 1), :].rearrange("p a d -> p (a d)"), h_ps[:, 0:D],
                                    base[:, bass.ds(t, 1), 0:D].rearrange("p a d -> p (a d)"), ALU.add).then_inc(h_done, 1)

                row_max(s * NT, 0)

                def body(t, g, par, first, last):
                    e = E[:, par, :]
                    link = Chain(s_search, g * (N_SEARCH))
                    search_begin(link, e, g, par)
                    descend(link, e, range(0, 4))
                    if not first:
                        new_features(t - 1, g - 1, 1 - par)
                    if not last:
                        row_max(g + 1, 1 - par)
                    descend(link, e, range(4, K))
                    if not first:
                        add_out(t - 1, g - 1)
                    search_end(link, e, g, par)
                    assert link.n == N_SEARCH, link.n
                over_tiles(dve, s, body)
                new_features(NT - 1, s * NT + NT - 1, (NT - 1) % 2)
                add_out(NT - 1, s * NT + NT - 1)

            link = Chain(s_fin, 0)
            dve.wait_ge(h_done, STEPS * NT)
            dve.wait_ge(w_loaded, 16 * (2 * STEPS + 5))

            def per_row(a):
                return a.rearrange("p (t a) -> p t a", a=1).to_broadcast([P, NT, D])

            sq = junk[:, 0:NT * D].rearrange("p (t d) -> p t d", t=NT)
            for n in range(2):
                link(v.tensor_reduce(mv[:, :], H[:, :, :], AX.X, ALU.add))
                link(v.tensor_scalar(mv[:, :], mv[:, :], 1.0 / D, None, ALU.mult))
                link(v.tensor_tensor(H[:, :, :], H[:, :, :], per_row(mv[:, :]), ALU.subtract))
                link(v.tensor_tensor(sq, H[:, :, :], H[:, :, :], ALU.mult))
                link(v.tensor_reduce(mv[:, :], sq, AX.X, ALU.add))
                v.tensor_scalar(sd[:, :], mv[:, :], 1.0 / D, LN_EPS, ALU.mult, ALU.add).then_inc(var_ready, 1)
                dve.wait_ge(sd_ready, n + 1)
                link(v.reciprocal(rs[:, :], sd[:, :]))
                if n == 0:
                    link(v.tensor_tensor(H[:, :, :], H[:, :, :], per_row(rs[:, :]), ALU.mult))
                    link(v.tensor_tensor(H[:, :, :], H[:, :, :], gb[:, 0:1, :].to_broadcast([P, NT, D]), ALU.mult))
                    link(v.tensor_tensor(H[:, :, :], H[:, :, :], gb[:, 1:2, :].to_broadcast([P, NT, D]), ALU.add))
                    link(v.tensor_tensor(H[:, :, :], H[:, :, :], X0[:, :, 0:D], ALU.add))
                else:
                    v.tensor_tensor(H[:, :, :], H[:, :, :], per_row(rs[:, :]), ALU.mult).then_inc(out_ready, 1)


_INS = ["x", "adj", "L0_gnn_W1", "L0_gnn_W2", "L0_gnn_W3", "L0_gnn_U1", "L0_gnn_U2", "L0_gnn_ln_g", "L0_gnn_ln_b"]


def kernel(**inputs):
    import numpy as _np
    import concourse.bacc as _bacc
    from concourse import mybir as _mybir
    from concourse.bass_utils import run_bass_kernel_spmd as _run

    nc = _bacc.Bacc("TRN2", target_bir_lowering=False, num_devices=1)
    arrays, args = {}, []
    for name in _INS:
        a = _np.ascontiguousarray(inputs[name])
        arrays[f"in_{name}_dram"] = a
        args.append(nc.dram_tensor(f"in_{name}_dram", a.shape, _mybir.dt.from_np(a.dtype), kind="ExternalInput").ap())
    shape, dtype = inputs["x"].shape, _mybir.dt.from_np(_np.dtype("float32"))
    args.append(nc.dram_tensor("out_0_dram", shape, dtype, kind="ExternalOutput").ap())
    gnn_top_p_kernel(nc, *args)
    r = _run(nc, [arrays], core_ids=[0])
    return r.results[0]["out_0_dram"]
```

```python
import concourse.bass as bass
from concourse import mybir
from contextlib import ExitStack
import numpy as np


def gnn_top_p_kernel(nc, x, adj, W1, W2, W3, U1, U2, ln_g, ln_b, out):
    fp32 = mybir.dt.float32
    bf16 = mybir.dt.bfloat16
    ALU = mybir.AluOpType
    ACT = mybir.ActivationFunctionType
    AX = mybir.AxisListType

    P = 128
    N, D = x.shape
    DA = W1.shape[0]
    STEPS = U1.shape[0]
    NT = (N + P - 1) // P
    LAST = N - (NT - 1) * P
    NP = NT * P
    BANK = 512
    CH = BANK // P
    NCH = (NT + CH - 1) // CH
    CW = [min(BANK, NP - c * BANK) for c in range(NCH)]
    LW = [min(BANK, N - c * BANK) for c in range(NCH)]
    LN_EPS = 1e-5
    DROP = float(np.float32(1.0) - np.float32(0.9))
    LOG_RANGE = float(np.log(NP / DROP) + 0.1)
    K_FIRST, K_NEXT = 9, 8
    W_FIRST, W_NEXT = 1, 3
    K_FULL = 42
    FACT = [float(np.exp(LOG_RANGE / 2 ** (k + 1))) for k in range(max(K_FIRST, K_NEXT))]
    SLACK = 2e-6
    AIM = 20.0
    RUN = [P] + [P // 4] * (STEPS - 1)
    NC = [NP // r * 8 for r in RUN]
    BIG = 1e30
    assert NT % 2 == 0

    ctx = ExitStack()
    with ctx:
        def sb(name, shape, dt=fp32):
            return ctx.enter_context(nc.sbuf_tensor(name, shape, dt))

        def pb(name):
            return ctx.enter_context(nc.psum_tensor(name, [P, BANK], fp32))

        def sem(name):
            return ctx.enter_context(nc.semaphore(name))

        X0 = sb("X0", [P, NT, D + 1])
        XF = sb("XF", [P, NT, D + 1])
        XA = sb("XA", [P, NT, D])
        H = sb("H", [P, NT, D])
        ident = sb("ident", [P, P])
        u_in = sb("u_in", [P, 2 * STEPS, D])
        w_in = sb("w_in", [DA, 2, D])
        w2_in = sb("w2_in", [DA, DA])
        UT = sb("UT", [P, 2 * STEPS, D])
        WT = sb("WT", [P, 2, DA])
        W2T = sb("W2T", [DA, DA])
        gb = sb("gb", [P, 2, D])
        xT = sb("xT", [P, 2, BANK])
        x1T = sb("x1T", [DA, BANK])
        kT = sb("kT", [DA, NP])
        qT = sb("qT", [DA, NP])
        q_tile = sb("q_tile", [DA, 2, P])
        E = sb("E", [P, 2, NP])
        junk = sb("junk", [P, NP])
        eq = sb("eq", [P, NP], bf16)
        A = sb("A", [P, NP])
        S = sb("S", [P, 2, NP])
        blkT = sb("blkT", [P, 2, BANK])
        newF = sb("newF", [P, D])
        newA = sb("newA", [P, D])
        newT = sb("newT", [P, 2, P])
        top8 = sb("top8", [P, 8])
        negm = sb("negm", [P, 2])
        cand = sb("cand", [P, 2, max(NC)])
        candW = sb("candW", [P, NT * 8])
        csum = sb("csum", [P, 2])
        junkC = sb("junkC", [P, max(NC)])
        flag_in = sb("flag_in", [P, 32])
        flag_T = sb("flag_T", [P, 32])
        flag_q = sb("flag_q", [P, 1])
        flag_4 = sb("flag_4", [1, 4])
        flag_i = sb("flag_i", [1, 1], mybir.dt.int32)
        mask_i = sb("mask_i", [P, 2], mybir.dt.int32)
        h_sb = sb("h_sb", [P, D])
        spare = sb("spare", [P, NCH])
        Z = sb("Z", [P, 2])
        st = sb("st", [P, 40])
        w8 = sb("w8", [P, 8])
        c8 = sb("c8", [P, 8])
        d8 = sb("d8", [P, 8])
        ones8 = sb("ones8", [P, 8])
        fin = sb("fin", [P, 4])
        den = sb("den", [P, 1])
        rinv = sb("rinv", [P, 1])
        mv = sb("mv", [P, NT])
        sd = sb("sd", [P, NT])
        rs = sb("rs", [P, NT])

        logit_ps = [pb("logit_ps0"), pb("logit_ps1")]
        blk_ps = [pb("blk_ps0"), pb("blk_ps1")]
        racc = pb("racc")
        aacc = pb("aacc")
        newT_ps = pb("newT_ps")
        h_ps = pb("h_ps")

        x_loaded = sem("x_loaded")
        w_loaded = sem("w_loaded")
        adj_loaded = [sem("adj_loaded0"), sem("adj_loaded1")]
        pool_step = sem("pool_step")
        setup_done = sem("setup_done")
        wT_ready = sem("wT_ready")
        wT_done = sem("wT_done")
        xT_ready = sem("xT_ready")
        xT_done = sem("xT_done")
        k_ready = sem("k_ready")
        k_done = sem("k_done")
        x1_ready = sem("x1_ready")
        x1_done = sem("x1_done")
        q_ready = sem("q_ready")
        q_done = sem("q_done")
        qt_ready = sem("qt_ready")
        logits_ready = sem("logits_ready")
        logits_done = sem("logits_done")
        max_ready = sem("max_ready")
        e_ready = sem("e_ready")
        a_ready = sem("a_ready")
        blk_ready = sem("blk_ready")
        blk_done = sem("blk_done")
        blk_used = sem("blk_used")
        new_ready = sem("new_ready")
        new_saved = sem("new_saved")
        newT_ready = sem("newT_ready")
        newT_done = sem("newT_done")
        h_ready = sem("h_ready")
        s_search = sem("s_search")
        s_level = sem("s_level")
        s_full = sem("s_full")
        s_final = sem("s_final")
        s_tie = sem("s_tie")
        diag_ready = sem("diag_ready")
        rinv_ready = sem("rinv_ready")
        h_copied = sem("h_copied")
        h_added = sem("h_added")
        s_max = sem("s_max")
        s_fin = sem("s_fin")
        var_ready = sem("var_ready")
        sd_ready = sem("sd_ready")
        out_ready = sem("out_ready")
        out_written = sem("out_written")

        block = ctx.enter_context(nc.Block())

        def over_tiles(eng, s, body):
            body(0, s * NT, 0, True, False)
            with eng.Fori(0, (NT - 2) // 2) as p:
                for j in (1, 2):
                    body(2 * p + j, 2 * p + (s * NT + j), j % 2, False, False)
            body(NT - 1, s * NT + NT - 1, (NT - 1) % 2, False, True)

        def over_tiles_ahead(eng, s, body):
            body(0, s * NT, 0, True, True, False)
            with eng.Fori(0, (NT - 4) // 2) as p:
                for j in (1, 2):
                    body(2 * p + j, 2 * p + (s * NT + j), j % 2, False, True, False)
            for t in range(NT - 3, NT):
                body(t, s * NT + t, t % 2, False, t + 2 < NT, t == NT - 1)

        @block.sync
        def _(sp):
            sp.dma_start(X0[:, 0:NT - 1, 0:D], x[0:(NT - 1) * P, :].rearrange("(t p) d -> p t d", p=P)).then_inc(x_loaded, 16)
            sp.dma_start(X0[0:LAST, NT - 1, 0:D], x[(NT - 1) * P:N, :]).then_inc(x_loaded, 16)
            sp.dma_start(X0[LAST:P, NT - 1, 0:D], x[0:P - LAST, :]).then_inc(x_loaded, 16)
            for n in range(STEPS):
                sp.dma_start(u_in[:, n, :], U1[n, :, :]).then_inc(w_loaded, 16)
                sp.dma_start(u_in[:, STEPS + n, :], U2[n, :, :]).then_inc(w_loaded, 16)
            sp.dma_start(w_in[:, 0, :], W1[:, :]).then_inc(w_loaded, 16)
            sp.dma_start(w_in[:, 1, :], W3[:, :]).then_inc(w_loaded, 16)
            sp.dma_start(w2_in[:, :], W2[:, :]).then_inc(w_loaded, 16)
            for n, v in enumerate((ln_g, ln_b)):
                sp.dma_start(gb[:, n, :], v.rearrange("(a d) -> a d", a=1).to_broadcast([P, D])).then_inc(w_loaded, 16)
            for s in range(STEPS):
                def load_pair(p, short):
                    for j in range(2):
                        g = 2 * p + (s * NT + j)
                        if not (s == 0 and isinstance(p, int) and p == 0):
                            sp.wait_ge(blk_ready, (g - 2) * (2 * NCH) + NCH)
                        r0 = (2 * p + j) * P
                        if short and j == 1:
                            m = LAST // 16 * 16
                            sp.dma_start(S[0:m, j, 0:N], adj[r0:r0 + m, :]).then_inc(adj_loaded[j], 16)
                            sp.dma_start(S[m:LAST, j, 0:N], adj[r0 + m:N, :]).then_inc(adj_loaded[j], 16)
                        else:
                            sp.dma_start(S[:, j, 0:N], adj[bass.ds(r0, P), :]).then_inc(adj_loaded[j], 16)
                load_pair(0, False)
                with sp.Fori(1, NT // 2 - 1) as p:
                    load_pair(p, False)
                load_pair(NT // 2 - 1, True)
            sp.wait_ge(out_ready, 1)
            sp.dma_start(out[0:(NT - 1) * P, :].rearrange("(t p) d -> p t d", p=P), H[:, 0:NT - 1, :]).then_inc(out_written, 16)
            sp.dma_start(out[(NT - 1) * P:N, :], H[0:LAST, NT - 1, :]).then_inc(out_written, 16)
            sp.wait_ge(out_written, 32)

        @block.gpsimd
        def _(pool):
            pool.memset(ident[:, :], 0.0).then_inc(pool_step, 1)
            pool.wait_ge(pool_step, 1)
            pool.affine_select(out=ident[:, :], in_=ident[:, :], compare_op=ALU.not_equal, fill=1.0,
                               base=0, pattern=[[-1, P]], channel_multiplier=1).then_inc(setup_done, 1)
            pool.memset(X0[:, :, D:D + 1], 1.0).then_inc(setup_done, 1)
            pool.memset(XF[:, :, D:D + 1], 1.0).then_inc(setup_done, 1)
            pool.memset(S[:, :, N:NP], 0.0).then_inc(setup_done, 1)
            pool.memset(E[:, :, N:NP], 0.0).then_inc(setup_done, 1)
            pool.memset(ones8[:, :], 1.0).then_inc(setup_done, 1)
            pool.memset(flag_in[:, :], 0.0).then_inc(setup_done, 1)
            pool.wait_ge(setup_done, 7)

            for s in range(STEPS):
                def fetch_q(t, g, par):
                    if s or not isinstance(t, int) or t >= 2:
                        pool.wait_ge(logits_ready, (g - 1) * NCH)
                    pool.tensor_copy(q_tile[:, par, :], qT[:, bass.ds(t * P, P)]).then_inc(qt_ready, 1)

                def add_diagonal(t, g, par, last):
                    pool.wait_ge(adj_loaded[par], 8 * g + (8 * (2 - par) + (16 * s if par else 0) + (16 if last else 0)))
                    w = LAST if last else P
                    d = S[:, par, bass.ds(t * P, w)]
                    pool.tensor_tensor(d, d, ident[:, 0:w], ALU.add).then_inc(diag_ready, 1)

                def save_new(t, g):
                    if s == 0:
                        pool.wait_ge(new_ready, g + 1)
                        pool.tensor_copy(XF[:, bass.ds(t, 1), 0:D], newF[:, :].rearrange("p (a d) -> p a d", a=1))
                        pool.tensor_copy(XA[:, bass.ds(t, 1), :], newA[:, :].rearrange("p (a d) -> p a d", a=1)).then_inc(new_saved, 1)

                def add_out(t, g):
                    base = X0 if s == 0 else H
                    pool.wait_ge(h_copied, g + 1)
                    pool.tensor_tensor(H[:, bass.ds(t, 1), :], h_sb[:, :].rearrange("p (a d) -> p a d", a=1),
                                       base[:, bass.ds(t, 1), 0:D], ALU.add).then_inc(h_added, 1)

                add_diagonal(0, s * NT, 0, False)
                pool.wait_ge(q_done, (s + 1) * NCH)
                fetch_q(0, s * NT, 0)
                fetch_q(1, s * NT + 1, 1)

                def body(t, g, par, first, last):
                    if not last:
                        fetch_q(t + 2, g + 2, par)
                        add_diagonal(t + 1, g + 1, 1 - par, False)
                    if not first:
                        save_new(t - 1, g - 1)
                        add_out(t - 1, g - 1)

                body(0, s * NT, 0, True, False)
                with pool.Fori(0, (NT - 2) // 2 - 1) as p:
                    for j in (1, 2):
                        body(2 * p + j, 2 * p + (s * NT + j), j % 2, False, False)
                t = NT - 3
                body_g = s * NT + t
                fetch_q(t + 2, body_g + 2, 1)
                add_diagonal(t + 1, body_g + 1, 0, False)
                save_new(t - 1, body_g - 1)
                add_out(t - 1, body_g - 1)
                t = NT - 2
                body_g = s * NT + t
                add_diagonal(t + 1, body_g + 1, 1, True)
                save_new(t - 1, body_g - 1)
                add_out(t - 1, body_g - 1)
                for t in (NT - 2, NT - 1):
                    save_new(t, s * NT + t)
                    add_out(t, s * NT + t)

        @block.tensor
        def _(pe):
            pe.wait_ge(setup_done, 1)
            pe.wait_ge(w_loaded, 16 * (2 * STEPS + 5))
            for n in range(2 * STEPS):
                pe.transpose(blk_ps[0][:, n * P:(n + 1) * P], u_in[:, n, :], ident[:, :])
            for n in range(2):
                pe.transpose(blk_ps[1][:, n * DA:(n + 1) * DA], w_in[:, n, :], ident[0:DA, 0:DA])
            pe.transpose(blk_ps[1][0:DA, 2 * DA:3 * DA], w2_in[:, :], ident[0:DA, 0:DA]).then_inc(wT_ready, 1)
            pe.wait_ge(wT_done, 3)
            pe.wait_ge(x_loaded, 48)

            for s in range(STEPS):
                Xf, Xa = (X0, X0) if s == 0 else (XF, XA)
                if s:
                    pe.wait_ge(new_saved, s * NT)
                for c in range(NCH):
                    n = s * NCH + c
                    w = CW[c]
                    if n >= 2:
                        pe.wait_ge(xT_done, n - 1)
                    for b in range(w // P):
                        last = pe.transpose(blk_ps[c % 2][:, b * P:(b + 1) * P], Xa[:, c * CH + b, 0:D], ident[:, :])
                    last.then_inc(xT_ready, 1)
                    pe.wait_ge(xT_done, n + 1)
                    if n:
                        pe.wait_ge(k_done, n)
                    pe.matmul(racc[0:DA, 0:w], WT[:, 1, :], xT[:, c % 2, 0:w], start=True, stop=True).then_inc(k_ready, 1)
                    if n:
                        pe.wait_ge(x1_done, n)
                    pe.matmul(aacc[0:DA, 0:w], WT[:, 0, :], xT[:, c % 2, 0:w], start=True, stop=True).then_inc(x1_ready, 1)
                    pe.wait_ge(x1_done, n + 1)
                    if n:
                        pe.wait_ge(q_done, n)
                    pe.matmul(newT_ps[0:DA, 0:w], W2T[:, :], x1T[:, 0:w], start=True, stop=True).then_inc(q_ready, 1)
                pe.wait_ge(k_done, (s + 1) * NCH)
                pe.wait_ge(q_done, (s + 1) * NCH)

                def logits(g, par):
                    pe.wait_ge(qt_ready, g + 1)
                    for c in range(NCH):
                        if not (isinstance(g, int) and g == 0 and c < 2):
                            pe.wait_ge(logits_done, g * NCH + (c - 1))
                        pe.matmul(logit_ps[(c + par) % 2][:, 0:LW[c]], q_tile[:, par, :],
                                  kT[:, c * BANK:c * BANK + LW[c]], start=True, stop=True).then_inc(logits_ready, 1)

                def product(src, rhs, width, acc, base, odd):
                    def turn(c):
                        if not (isinstance(base, int) and base + c < 2):
                            pe.wait_ge(blk_done, base + (c - 1))
                        for b in range(CW[c] // P):
                            j = c * CH + b
                            m = pe.transpose(blk_ps[(c + odd) % 2][:, b * P:(b + 1) * P], src[:, j * P:(j + 1) * P], ident[:, :])
                        m.then_inc(blk_ready, 1)
                    turn(0)
                    for c in range(NCH):
                        if c + 1 < NCH:
                            turn(c + 1)
                        pe.wait_ge(blk_done, base + (c + 1))
                        for b in range(CW[c] // P):
                            j = c * CH + b
                            m = pe.matmul(acc[:, 0:width], blkT[:, (c + odd) % 2, b * P:(b + 1) * P], rhs[:, j, 0:width],
                                          start=(j == 0), stop=(j == NT - 1))
                        m.then_inc(blk_used, 1)

                def tile_out(g):
                    pe.wait_ge(new_ready, g + 1)
                    if not (isinstance(g, int) and g == 0):
                        pe.wait_ge(newT_done, g)
                    pe.transpose(newT_ps[:, 0:P], newF[:, :], ident[:, :])
                    pe.transpose(newT_ps[:, P:2 * P], newA[:, :], ident[:, :]).then_inc(newT_ready, 1)
                    pe.wait_ge(newT_done, g + 1)
                    if not (isinstance(g, int) and g == 0):
                        pe.wait_ge(h_copied, g)
                    pe.matmul(h_ps[:, 0:D], newT[:, 0, :], UT[:, s, :], start=True, stop=False)
                    pe.matmul(h_ps[:, 0:D], newT[:, 1, :], UT[:, STEPS + s, :], start=False, stop=True).then_inc(h_ready, 1)

                logits(s * NT, 0)
                logits(s * NT + 1, 1)

                def body(t, g, par, first, two_more, last):
                    pe.wait_ge(diag_ready, g + 1)
                    if not (isinstance(g, int) and g == 0):
                        pe.wait_ge(new_ready, g)
                    product(S[:, par, :], Xf, D + 1, racc, g * (2 * NCH), 0)
                    if not first:
                        tile_out(g - 1)
                    if two_more:
                        logits(g + 2, par)
                    pe.wait_ge(a_ready, g + 1)
                    product(A, Xa, D, aacc, g * (2 * NCH) + NCH, NCH % 2)
                over_tiles_ahead(pe, s, body)
                tile_out(s * NT + NT - 1)

        @block.scalar
        def _(act):
            act.wait_ge(wT_ready, 1)
            act.activation(UT[:, :, :], blk_ps[0][:, :].rearrange("p (n d) -> p n d", n=2 * STEPS), ACT.Copy).then_inc(wT_done, 1)
            act.activation(WT[:, :, :], blk_ps[1][:, 0:2 * DA].rearrange("p (n d) -> p n d", n=2), ACT.Copy).then_inc(wT_done, 1)
            act.activation(W2T[:, :], blk_ps[1][0:DA, 2 * DA:3 * DA], ACT.Copy).then_inc(wT_done, 1)
            act.wait_ge(setup_done, 6)
            for s in range(STEPS):
                for c in range(NCH):
                    n = s * NCH + c
                    act.wait_ge(xT_ready, n + 1)
                    if n >= 2:
                        act.wait_ge(x1_ready, n - 1)
                    act.activation(xT[:, c % 2, 0:CW[c]], blk_ps[c % 2][:, 0:CW[c]], ACT.Copy).then_inc(xT_done, 1)
                    act.wait_ge(x1_ready, n + 1)
                    if n:
                        act.wait_ge(q_ready, n)
                    act.activation(x1T[:, 0:CW[c]], aacc[0:DA, 0:CW[c]], ACT.Copy).then_inc(x1_done, 1)

                def store_logits(g, par):
                    if not (isinstance(g, int) and g < 2):
                        act.wait_ge(a_ready, g - 1)
                    for c in range(NCH):
                        act.wait_ge(logits_ready, g * NCH + (c + 1))
                        act.activation(E[:, par, c * BANK:c * BANK + LW[c]], logit_ps[(c + par) % 2][:, 0:LW[c]],
                                       ACT.Copy).then_inc(logits_done, 1)

                def exponentials(g, par):
                    act.wait_ge(max_ready, g + 1)
                    act.activation(cand[:, par, 0:NC[s]], cand[:, par, 0:NC[s]], ACT.Exp, bias=negm[:, par:par + 1], scale=1.0,
                                   accum_out=csum[:, par:par + 1])
                    act.activation(E[:, par, 0:N], E[:, par, 0:N], ACT.Exp, bias=negm[:, par:par + 1], scale=1.0,
                                   accum_out=Z[:, par:par + 1]).then_inc(e_ready, 1)

                def empty_blocks(base, odd):
                    for c in range(NCH):
                        act.wait_ge(blk_ready, base + (c + 1))
                        if not (isinstance(base, int) and base + c < 2):
                            act.wait_ge(blk_used, base + (c - 1))
                        act.activation(blkT[:, (c + odd) % 2, 0:CW[c]], blk_ps[(c + odd) % 2][:, 0:CW[c]],
                                       ACT.Copy).then_inc(blk_done, 1)

                def empty_new(g):
                    act.wait_ge(newT_ready, g + 1)
                    if not (isinstance(g, int) and g == 0):
                        act.wait_ge(h_ready, g)
                    act.activation(newT[:, :, :], newT_ps[:, 0:2 * P].rearrange("p (n d) -> p n d", n=2),
                                   ACT.Copy).then_inc(newT_done, 1)

                def new_features(g):
                    if not (isinstance(g, int) and g == 0):
                        act.wait_ge(newT_ready, g)
                        if s == 0:
                            act.wait_ge(new_saved, g)
                    act.wait_ge(rinv_ready, g + 1)
                    act.activation(newF[:, :], racc[:, 0:D], ACT.Copy, scale=rinv[:, 0:1])
                    act.wait_ge(a_ready, g + 1)
                    act.wait_ge(blk_used, (g + 1) * (2 * NCH))
                    act.activation(newA[:, :], aacc[:, 0:D], ACT.Copy, scale=den[:, 0:1]).then_inc(new_ready, 1)

                def store_out(g):
                    act.wait_ge(h_ready, g + 1)
                    if not (isinstance(g, int) and g == 0):
                        act.wait_ge(h_added, g)
                    act.activation(h_sb[:, :], h_ps[:, 0:D], ACT.Copy).then_inc(h_copied, 1)

                store_logits(s * NT, 0)
                exponentials(s * NT, 0)
                store_logits(s * NT + 1, 1)

                def body(t, g, par, first, two_more, last):
                    if not first:
                        new_features(g - 1)
                    empty_blocks(g * (2 * NCH), 0)
                    if not first:
                        empty_new(g - 1)
                        store_out(g - 1)
                    if not last:
                        exponentials(g + 1, 1 - par)
                    if two_more:
                        store_logits(g + 2, par)
                    empty_blocks(g * (2 * NCH) + NCH, NCH % 2)
                over_tiles_ahead(act, s, body)
                new_features(s * NT + NT - 1)
                empty_new(s * NT + NT - 1)
                store_out(s * NT + NT - 1)
            for n in range(2):
                act.wait_ge(var_ready, n + 1)
                act.activation(sd[:, :], sd[:, :], ACT.Sqrt).then_inc(sd_ready, 1)

        @block.vector
        def _(dve):
            v = nc.vector
            class Chain:
                def __init__(self, sem, others=(), skip=0):
                    self.sem, self.n, self.others, self.skip = sem, 0, others, skip
                    dve.sem_clear(sem)

                def post(self, ins):
                    self.n += 1
                    ins.then_inc(self.sem, 1)

                def __call__(self, ins):
                    self.post(ins)
                    if self.others and self.n > self.skip:
                        self.others.pop(0)()
                    dve.wait_ge(self.sem, self.n)

            SKIP = 7

            def col(n, m=1):
                return st[:, n:n + m]

            (DROPZ, THR, LOW, PICK, LOWW, ROOM, TSTAR, GAP, TIE, SLOW, S2, FLAG, FLOOR, BUDGET, THRLO, THRHI,
             LO, HI, RLO, RHI, WIDTH, FRAC, T2, L2, CSW, SGT, TIES, KEPT, MASS, STEP, ONE) = range(31)

            def pick_smallest_kept(link, w, room):
                link(v.tensor_tensor_scan(c8[:, :], ones8[:, :], w8[:, :], 0.0, ALU.mult, ALU.add))
                link(v.tensor_tensor(d8[:, :], c8[:, :], w8[:, :], ALU.subtract))
                link(v.tensor_scalar(d8[:, :], d8[:, :], col(room), BIG, ALU.is_ge, ALU.mult))
                link(v.tensor_tensor(d8[:, :], d8[:, :], w8[:, :], ALU.max))
                link(v.tensor_reduce(col(TSTAR), d8[:, :], AX.X, ALU.min))

            def search(link, c, mass, csum, n_trials, n_looks):
                fact = FACT[:n_trials]
                link(v.scalar_tensor_tensor(out=col(BUDGET), in0=csum, scalar=mass, in1=col(DROPZ),
                                            op0=ALU.subtract, op1=ALU.add))
                link(v.tensor_scalar(col(THR), col(DROPZ), fact[0] / NP, None, ALU.mult))
                for k in range(n_trials):
                    nxt = fact[k + 1] if k + 1 < n_trials else 1.0
                    link(v.scalar_tensor_tensor(out=junkC[:, 0:c.shape[1]], in0=c, scalar=col(THR), in1=c, op0=ALU.is_lt,
                                                op1=ALU.mult, accum_out=col(LOW)))
                    link(v.tensor_scalar(col(PICK), col(LOW), col(BUDGET), nxt - nxt / fact[k], ALU.is_le, ALU.mult))
                    link(v.scalar_tensor_tensor(out=col(THR), in0=col(PICK), scalar=nxt / fact[k], in1=col(THR),
                                                op0=ALU.add, op1=ALU.mult))
                link.post(v.tensor_scalar(col(THRLO), col(THR), 1.0 - SLACK, None, ALU.mult))
                link(v.tensor_scalar(col(THRHI), col(THR), fact[-1] * (1.0 + SLACK), None, ALU.mult))
                link(v.scalar_tensor_tensor(out=junkC[:, 0:c.shape[1]], in0=c, scalar=col(THRHI), in1=c, op0=ALU.is_lt,
                                            op1=ALU.mult, accum_out=col(LOWW)))
                link.post(v.tensor_tensor(col(ROOM), col(LOWW), col(BUDGET), ALU.subtract))
                link.post(v.max(w8[:, :], junkC[:, 0:c.shape[1]]))
                link(v.tensor_reduce(col(FLOOR), c.rearrange("p (n k) -> p n k", k=8)[:, :, 7], AX.X, ALU.max))
                pick_smallest_kept(link, w8, ROOM)
                for look in range(n_looks):
                    if look:
                        link.post(v.tensor_copy(col(PICK), col(TSTAR)))
                        link(v.max(w8[:, :], junkC[:, 0:c.shape[1]]))
                        pick_smallest_kept(link, w8, GAP)
                        link(v.tensor_tensor(col(TSTAR), col(TSTAR), col(PICK), ALU.min))
                    link(v.scalar_tensor_tensor(out=junkC[:, 0:c.shape[1]], in0=c, scalar=col(TSTAR), in1=c, op0=ALU.is_lt,
                                                op1=ALU.mult, accum_out=col(LOW)))
                    link(v.tensor_tensor(col(GAP), col(LOW), col(BUDGET), ALU.subtract))
                link.post(v.tensor_scalar(col(SLOW), col(GAP), 0.0, None, ALU.is_gt))
                link.post(v.tensor_scalar(col(S2), col(TSTAR), 2.0, None, ALU.is_gt))
                link(v.tensor_scalar(col(TIE), col(GAP), col(TSTAR), 0.0, ALU.add, ALU.is_le))
                link(v.tensor_tensor(col(SLOW), col(SLOW), col(S2), ALU.max))
                link(v.tensor_scalar(col(S2), col(TSTAR), col(FLOOR), None, ALU.is_le))
                link(v.tensor_tensor(col(SLOW), col(SLOW), col(S2), ALU.max))
                link(v.scalar_tensor_tensor(out=flag_in[:, 0:1], in0=col(SLOW), scalar=2.0, in1=col(TIE),
                                            op0=ALU.mult, op1=ALU.add))

            def reduce_flag(link):
                link(v.transpose(flag_T[:, :], flag_in[:, :]))
                link(v.tensor_reduce(flag_q[:, :], flag_T[:, :], AX.X, ALU.max))
                for q in range(4):
                    ins = v.tensor_copy(flag_4[0:1, q:q + 1], flag_q[32 * q:32 * q + 1, :])
                    (link if q == 3 else link.post)(ins)
                link(v.tensor_reduce(flag_i[:, :], flag_4[:, :], AX.X, ALU.max))

            def where(link, dst, mask, src):
                link.post(v.copy_predicated(col(dst), mask_i[:, mask:mask + 1], src if not isinstance(src, int) else col(src)))

            def evaluate(link, e, t):
                link(v.scalar_tensor_tensor(out=junk[:, :], in0=e, scalar=col(t), in1=e, op0=ALU.is_lt,
                                            op1=ALU.mult, accum_out=col(L2)))
                link.post(v.tensor_scalar(mask_i[:, 0:1], col(L2), col(DROPZ), None, ALU.is_le))
                link(v.tensor_scalar(mask_i[:, 1:2], col(L2), col(DROPZ), None, ALU.is_gt))

            def settle(link):
                link(v.tensor_scalar(mask_i[:, 0:1], col(SLOW), 0.0, None, ALU.is_equal))
                link(v.tensor_scalar(col(T2), col(TSTAR), 1.0 + 3e-7, None, ALU.mult))
                where(link, LO, 0, TSTAR)
                link(v.copy_predicated(col(HI), mask_i[:, 0:1], col(T2)))

            def mass_below_hi(link, c, mass, csum, out):
                link(v.scalar_tensor_tensor(out=junkC[:, 0:c.shape[1]], in0=c, scalar=col(HI), in1=c, op0=ALU.is_lt,
                                            op1=ALU.mult, accum_out=col(LOW)))
                link(v.tensor_tensor(col(out), col(LOW), csum, ALU.subtract))
                link(v.tensor_tensor(col(out), col(out), mass, ALU.add))

            def first_bracket(link, c, par):
                link.post(v.tensor_copy(col(LO), col(THRLO)))
                link.post(v.tensor_copy(col(RLO), col(DROPZ)))
                link(v.tensor_scalar(col(HI), col(FLOOR), 1.0 + SLACK, col(THRHI), ALU.mult, ALU.max))
                mass_below_hi(link, c, Z[:, par:par + 1], csum[:, par:par + 1], RHI)
                settle(link)

            def next_bracket(link):
                link(v.tensor_tensor(col(THRLO), col(THRLO), col(T2), ALU.min))
                link(v.tensor_tensor(col(LO), col(LO), col(THRLO), ALU.max))
                link(v.tensor_scalar(col(FRAC), col(FLOOR), 1.0 + SLACK, col(THRHI), ALU.mult, ALU.max))
                link(v.tensor_tensor(col(FRAC), col(FRAC), col(T2), ALU.min))
                where(link, HI, 1, FRAC)
                where(link, RLO, 0, L2)
                link(v.tensor_copy(col(WIDTH), col(RHI)))
                mass_below_hi(link, candW[:, :], col(L2), col(CSW), WIDTH)
                link(v.copy_predicated(col(RHI), mask_i[:, 1:2], col(WIDTH)))
                settle(link)

            def level(link, e):
                link(v.tensor_tensor(col(WIDTH), col(HI), col(LO), ALU.subtract))
                link(v.scalar_tensor_tensor(out=col(T2), in0=col(WIDTH), scalar=0.1, in1=col(LO), op0=ALU.mult, op1=ALU.add))
                evaluate(link, e, T2)
                where(link, LO, 0, T2)
                where(link, RLO, 0, L2)
                where(link, HI, 1, T2)
                link(v.copy_predicated(col(RHI), mask_i[:, 1:2], col(L2)))
                link.post(v.tensor_tensor(col(WIDTH), col(HI), col(LO), ALU.subtract))
                link.post(v.scalar_tensor_tensor(out=col(FRAC), in0=col(HI), scalar=-AIM, in1=col(RHI), op0=ALU.mult, op1=ALU.add))
                link(v.tensor_tensor(col(T2), col(RHI), col(RLO), ALU.subtract))
                link(v.tensor_scalar(col(T2), col(T2), 1e-20, None, ALU.max))
                link.post(v.reciprocal(col(T2), col(T2)))
                link(v.tensor_tensor(col(FRAC), col(FRAC), col(DROPZ), ALU.subtract))
                link(v.tensor_tensor(col(FRAC), col(FRAC), col(T2), ALU.mult))
                link(v.tensor_scalar(col(FRAC), col(FRAC), 0.1, 0.9, ALU.max, ALU.min))
                link(v.tensor_tensor(col(FRAC), col(FRAC), col(SLOW), ALU.mult))
                link(v.tensor_tensor(col(WIDTH), col(WIDTH), col(FRAC), ALU.mult))
                link(v.tensor_tensor(col(T2), col(HI), col(WIDTH), ALU.subtract))
                evaluate(link, e, T2)
                for n in range(NT):
                    link.post(v.max(candW[:, 8 * n:8 * n + 8], junk[:, n * P:(n + 1) * P]))
                link(v.tensor_copy(col(ONE), col(L2)))
                link(v.tensor_reduce(col(CSW), candW[:, :], AX.X, ALU.add))
                search(link, candW[:, :], col(L2), col(CSW), K_NEXT, W_NEXT)
                reduce_flag(link)

            def full(e):
                link = Chain(s_full)
                link.post(v.memset(col(LO), 0.0))
                link(v.memset(col(STEP), 1.0))
                with dve.Fori(0, K_FULL) as k:
                    link = Chain(s_full)
                    link(v.tensor_tensor(col(THR), col(LO), col(STEP), ALU.add))
                    link(v.scalar_tensor_tensor(out=junk[:, :], in0=e, scalar=col(THR), in1=e, op0=ALU.is_lt,
                                                op1=ALU.mult, accum_out=col(LOW)))
                    link(v.tensor_scalar(col(PICK), col(LOW), col(DROPZ), None, ALU.is_le))
                    link(v.scalar_tensor_tensor(out=col(LO), in0=col(PICK), scalar=col(STEP), in1=col(LO), op0=ALU.mult, op1=ALU.add))
                    link(v.tensor_scalar(col(STEP), col(STEP), 0.5, None, ALU.mult))
                link = Chain(s_full)
                link(v.scalar_tensor_tensor(out=col(THRHI), in0=col(STEP), scalar=4.0, in1=col(LO), op0=ALU.mult, op1=ALU.add))
                link(v.tensor_scalar(col(THRHI), col(THRHI), 1.0 + SLACK, None, ALU.mult))
                link(v.scalar_tensor_tensor(out=junk[:, :], in0=e, scalar=col(THRHI), in1=e, op0=ALU.is_lt,
                                            op1=ALU.mult, accum_out=col(LOWW)))
                link.post(v.tensor_tensor(col(ROOM), col(LOWW), col(DROPZ), ALU.subtract))
                link(v.max(w8[:, :], junk[:, :]))
                pick_smallest_kept(link, w8, ROOM)
                link(v.memset(flag_i[:, :], 1))

            def load_flag():
                return dve.value_load(flag_i[0:1, 0:1], min_val=0, max_val=3)

            for s in range(STEPS):
                for c in range(NCH):
                    n = s * NCH + c
                    dve.wait_ge(k_ready, n + 1)
                    v.tensor_copy(kT[:, c * BANK:c * BANK + CW[c]], racc[0:DA, 0:CW[c]]).then_inc(k_done, 1)
                    dve.wait_ge(q_ready, n + 1)
                    v.tensor_copy(qT[:, c * BANK:c * BANK + CW[c]], newT_ps[0:DA, 0:CW[c]]).then_inc(q_done, 1)

                def candidates(g, par):
                    def run(n):
                        c, r = n * RUN[s] // BANK, RUN[s]
                        if n * r % BANK == 0:
                            dve.wait_ge(logits_done, g * NCH + (c + 1))
                            v.memset(spare[:, c:c + 1], 0.0)
                        m = v.max(cand[:, par, 8 * n:8 * n + 8], E[:, par, n * r:min((n + 1) * r, N)])
                        if (n + 1) * r == NP:
                            m.then_inc(s_max, 1)
                    return [lambda n=n: run(n) for n in range(NP // RUN[s])]

                def maxima(par):
                    dve.wait_ge(s_max, 1)
                    v.tensor_reduce(negm[:, par:par + 1], cand[:, par, 0:NC[s]], AX.X, ALU.max).then_inc(s_max, 1)
                    dve.wait_ge(s_max, 2)
                    v.tensor_scalar(negm[:, par:par + 1], negm[:, par:par + 1], -1.0, None, ALU.mult).then_inc(max_ready, 1)

                dve.sem_clear(s_max)
                for step in candidates(s * NT, 0):
                    step()
                maxima(0)

                def body(t, g, par, first, last):
                    e = E[:, par, :]
                    z = Z[:, par:par + 1]
                    others = [] if last else candidates(g + 1, 1 - par)
                    dve.sem_clear(s_max)
                    link = Chain(s_search, others, SKIP)
                    dve.wait_ge(e_ready, g + 1)
                    link(v.tensor_scalar(col(DROPZ), z, DROP, None, ALU.mult))
                    search(link, cand[:, par, 0:NC[s]], z, csum[:, par:par + 1], K_FIRST, W_FIRST)
                    reduce_flag(link)
                    for step in others:
                        step()
                    if not last:
                        maxima(1 - par)

                    with dve.If(load_flag() > 1):
                        link = Chain(s_level)
                        first_bracket(link, cand[:, par, 0:NC[s]], par)
                        level(link, e)
                        with dve.If(load_flag() > 1):
                            link = Chain(s_level)
                            next_bracket(link)
                            level(link, e)
                            with dve.If(load_flag() > 1):
                                full(e)

                    def last_tile_used():
                        if not (isinstance(g, int) and g == 0):
                            dve.wait_ge(new_ready, g)

                    with dve.If(load_flag() > 0):
                        link = Chain(s_tie)
                        last_tile_used()
                        link(v.scalar_tensor_tensor(out=A[:, :], in0=e, scalar=col(TSTAR), in1=e, op0=ALU.is_gt,
                                                    op1=ALU.mult, accum_out=col(SGT)))
                        link(v.tensor_tensor(col(TIES), z, col(SGT), ALU.subtract))
                        link(v.reciprocal(col(MASS), col(TSTAR)))
                        link(v.scalar_tensor_tensor(out=col(TIES), in0=col(TIES), scalar=col(DROPZ), in1=col(MASS),
                                                    op0=ALU.subtract, op1=ALU.mult))
                        link(v.tensor_scalar(col(TIES), col(TIES), 0.5, 1.0, ALU.max, ALU.add))
                        link(v.tensor_scalar(eq[:, :], e, col(TSTAR), None, ALU.is_equal))
                        link(v.tensor_tensor_scan(junk[:, :], eq[:, :], eq[:, :], 0.0, ALU.add, ALU.max))
                        link(v.scalar_tensor_tensor(out=eq[:, :], in0=junk[:, :], scalar=col(TIES), in1=eq[:, :],
                                                    op0=ALU.is_lt, op1=ALU.mult, accum_out=col(KEPT)))
                        link(v.scalar_tensor_tensor(out=col(MASS), in0=col(KEPT), scalar=col(TSTAR), in1=col(SGT),
                                                    op0=ALU.mult, op1=ALU.add))
                        link(v.scalar_tensor_tensor(out=A[:, :], in0=eq[:, :], scalar=col(TSTAR), in1=A[:, :],
                                                    op0=ALU.mult, op1=ALU.add))
                    with dve.Else():
                        link = Chain(s_tie)
                        last_tile_used()
                        link(v.scalar_tensor_tensor(out=A[:, :], in0=e, scalar=col(TSTAR), in1=e, op0=ALU.is_ge,
                                                    op1=ALU.mult, accum_out=col(MASS)))
                    link = Chain(s_final)
                    link(v.scalar_tensor_tensor(out=col(MASS), in0=z, scalar=1e-12, in1=col(MASS), op0=ALU.mult, op1=ALU.max))
                    v.reciprocal(den[:, :], col(MASS)).then_inc(a_ready, 1)
                    dve.wait_ge(blk_used, g * (2 * NCH) + NCH)
                    v.reciprocal(rinv[:, :], racc[:, D:D + 1]).then_inc(rinv_ready, 1)
                over_tiles(dve, s, body)

            link = Chain(s_fin)
            dve.wait_ge(h_added, STEPS * NT)
            dve.wait_ge(w_loaded, 16 * (2 * STEPS + 5))

            def per_row(a):
                return a.rearrange("p (t a) -> p t a", a=1).to_broadcast([P, NT, D])

            sq = junk[:, 0:NT * D].rearrange("p (t d) -> p t d", t=NT)
            for n in range(2):
                link(v.tensor_reduce(mv[:, :], H[:, :, :], AX.X, ALU.add))
                link(v.tensor_scalar(mv[:, :], mv[:, :], 1.0 / D, None, ALU.mult))
                link(v.tensor_tensor(H[:, :, :], H[:, :, :], per_row(mv[:, :]), ALU.subtract))
                link(v.tensor_tensor(sq, H[:, :, :], H[:, :, :], ALU.mult))
                link(v.tensor_reduce(mv[:, :], sq, AX.X, ALU.add))
                v.tensor_scalar(sd[:, :], mv[:, :], 1.0 / D, LN_EPS, ALU.mult, ALU.add).then_inc(var_ready, 1)
                dve.wait_ge(sd_ready, n + 1)
                link(v.reciprocal(rs[:, :], sd[:, :]))
                if n == 0:
                    link(v.tensor_tensor(H[:, :, :], H[:, :, :], per_row(rs[:, :]), ALU.mult))
                    link(v.tensor_tensor(H[:, :, :], H[:, :, :], gb[:, 0:1, :].to_broadcast([P, NT, D]), ALU.mult))
                    link(v.tensor_tensor(H[:, :, :], H[:, :, :], gb[:, 1:2, :].to_broadcast([P, NT, D]), ALU.add))
                    link(v.tensor_tensor(H[:, :, :], H[:, :, :], X0[:, :, 0:D], ALU.add))
                else:
                    v.tensor_tensor(H[:, :, :], H[:, :, :], per_row(rs[:, :]), ALU.mult).then_inc(out_ready, 1)


_INS = ["x", "adj", "L0_gnn_W1", "L0_gnn_W2", "L0_gnn_W3", "L0_gnn_U1", "L0_gnn_U2", "L0_gnn_ln_g", "L0_gnn_ln_b"]


def kernel(**inputs):
    import numpy as _np
    import concourse.bacc as _bacc
    from concourse import mybir as _mybir
    from concourse.bass_utils import run_bass_kernel_spmd as _run

    nc = _bacc.Bacc("TRN2", target_bir_lowering=False, num_devices=1)
    arrays, args = {}, []
    for name in _INS:
        a = _np.ascontiguousarray(inputs[name])
        arrays[f"in_{name}_dram"] = a
        args.append(nc.dram_tensor(f"in_{name}_dram", a.shape, _mybir.dt.from_np(a.dtype), kind="ExternalInput").ap())
    shape, dtype = inputs["x"].shape, _mybir.dt.from_np(_np.dtype("float32"))
    args.append(nc.dram_tensor("out_0_dram", shape, dtype, kind="ExternalOutput").ap())
    gnn_top_p_kernel(nc, *args)
    r = _run(nc, [arrays], core_ids=[0])
    return r.results[0]["out_0_dram"]
```

```python
import concourse.bass as bass
from concourse import mybir
from contextlib import ExitStack
import numpy as np


def gnn_top_p_kernel(nc, x, adj, W1, W2, W3, U1, U2, ln_g, ln_b, out):
    fp32 = mybir.dt.float32
    bf16 = mybir.dt.bfloat16
    ALU = mybir.AluOpType
    ACT = mybir.ActivationFunctionType
    AX = mybir.AxisListType

    P = 128
    N, D = x.shape
    DA = W1.shape[0]
    STEPS = U1.shape[0]
    NT = (N + P - 1) // P
    LAST = N - (NT - 1) * P
    NP = NT * P
    BANK = 512
    CH = BANK // P
    NCH = (NT + CH - 1) // CH
    CW = [min(BANK, NP - c * BANK) for c in range(NCH)]
    LW = [min(BANK, N - c * BANK) for c in range(NCH)]
    LN_EPS = 1e-5
    DROP = float(np.float32(1.0) - np.float32(0.9))
    LOG_RANGE = float(np.log(NP / DROP) + 0.1)
    K_FIRST, K_NEXT = 9, 7
    W_FIRST, W_NEXT = 1, 2
    K_FULL = 42
    FACT = [float(np.exp(LOG_RANGE / 2 ** (k + 1))) for k in range(max(K_FIRST, K_NEXT))]
    SLACK = 2e-6
    AIM = 20.0
    RUN = [P] + [P // 4] * (STEPS - 1)
    NC = [NP // r * 8 for r in RUN]
    BIG = 1e30
    assert NT % 2 == 0

    ctx = ExitStack()
    with ctx:
        def sb(name, shape, dt=fp32):
            return ctx.enter_context(nc.sbuf_tensor(name, shape, dt))

        def pb(name):
            return ctx.enter_context(nc.psum_tensor(name, [P, BANK], fp32))

        def sem(name):
            return ctx.enter_context(nc.semaphore(name))

        X0 = sb("X0", [P, NT, D + 1])
        XF = sb("XF", [P, NT, D + 1])
        XA = sb("XA", [P, NT, D + 1])
        H = sb("H", [P, NT, D])
        ident = sb("ident", [P, P])
        u_in = sb("u_in", [P, 2 * STEPS, D])
        w_in = sb("w_in", [DA, 2, D])
        w2_in = sb("w2_in", [DA, DA])
        UT = sb("UT", [P, 2 * STEPS, D])
        WT = sb("WT", [P, 2, DA])
        W2T = sb("W2T", [DA, DA])
        gb = sb("gb", [P, 2, D])
        xT = sb("xT", [P, 2, BANK])
        x1T = sb("x1T", [DA, BANK])
        kT = sb("kT", [DA, NP])
        qT = sb("qT", [DA, NP])
        q_tile = sb("q_tile", [DA, 2, P])
        E = sb("E", [P, 2, NP])
        junk = sb("junk", [P, NP])
        eq = sb("eq", [P, NP], bf16)
        A = sb("A", [P, NP])
        S = sb("S", [P, 2, NP])
        blkT = sb("blkT", [P, 2, BANK])
        sumF = sb("sumF", [P, D + 1])
        sumA = sb("sumA", [P, D + 1])
        least = sb("least", [P, 2])
        newF = sb("newF", [P, D])
        newA = sb("newA", [P, D])
        newT = sb("newT", [P, 2, P])
        negm = sb("negm", [P, 2])
        cand = sb("cand", [P, 2, max(NC)])
        candW = sb("candW", [P, NT * 8])
        csum = sb("csum", [P, 2])
        junkC = sb("junkC", [P, max(NC)])
        flag_in = sb("flag_in", [P, 32])
        flag_T = sb("flag_T", [P, 32])
        flag_q = sb("flag_q", [P, 1])
        flag_4 = sb("flag_4", [1, 4])
        flag_i = sb("flag_i", [1, 1], mybir.dt.int32)
        mask_i = sb("mask_i", [P, 2], mybir.dt.int32)
        h_sb = sb("h_sb", [P, D])
        spare_pool = sb("spare_pool", [P, 1])
        spare = sb("spare", [P, NCH])
        Z = sb("Z", [P, 2])
        st = sb("st", [P, 40])
        w8 = sb("w8", [P, 8])
        c8 = sb("c8", [P, 8])
        d8 = sb("d8", [P, 8])
        ones8 = sb("ones8", [P, 8])
        den = sb("den", [P, 1])
        inv = sb("inv", [P, 2])
        mv = sb("mv", [P, NT])
        sd = sb("sd", [P, NT])
        rs = sb("rs", [P, NT])

        logit_ps = [pb("logit_ps0"), pb("logit_ps1")]
        blk_ps = [pb("blk_ps0"), pb("blk_ps1")]
        racc = pb("racc")
        aacc = pb("aacc")
        newT_ps = pb("newT_ps")
        h_ps = pb("h_ps")

        x_loaded = sem("x_loaded")
        w_loaded = sem("w_loaded")
        adj_loaded = [sem("adj_loaded0"), sem("adj_loaded1")]
        pool_step = sem("pool_step")
        setup_done = sem("setup_done")
        wT_ready = sem("wT_ready")
        wT_done = sem("wT_done")
        xT_ready = sem("xT_ready")
        xT_done = sem("xT_done")
        k_ready = sem("k_ready")
        k_done = sem("k_done")
        x1_ready = sem("x1_ready")
        x1_done = sem("x1_done")
        q_ready = sem("q_ready")
        q_done = sem("q_done")
        qt_ready = sem("qt_ready")
        logits_ready = sem("logits_ready")
        logits_done = sem("logits_done")
        max_ready = sem("max_ready")
        e_ready = sem("e_ready")
        a_ready = sem("a_ready")
        blk_ready = sem("blk_ready")
        blk_done = sem("blk_done")
        blk_used = sem("blk_used")
        new_ready = sem("new_ready")
        new_saved = sem("new_saved")
        newT_ready = sem("newT_ready")
        newT_done = sem("newT_done")
        h_ready = sem("h_ready")
        s_search = sem("s_search")
        s_level = sem("s_level")
        s_full = sem("s_full")
        s_tie = sem("s_tie")
        diag_ready = sem("diag_ready")
        sums_ready = sem("sums_ready")
        inv_ready = sem("inv_ready")
        h_copied = sem("h_copied")
        h_added = sem("h_added")
        s_max = sem("s_max")
        s_fin = sem("s_fin")
        var_ready = sem("var_ready")
        sd_ready = sem("sd_ready")
        out_ready = sem("out_ready")
        out_written = sem("out_written")

        block = ctx.enter_context(nc.Block())

        def over_tiles(eng, s, body):
            body(0, s * NT, 0, True, False)
            with eng.Fori(0, (NT - 2) // 2) as p:
                for j in (1, 2):
                    body(2 * p + j, 2 * p + (s * NT + j), j % 2, False, False)
            body(NT - 1, s * NT + NT - 1, (NT - 1) % 2, False, True)

        def over_tiles_ahead(eng, s, body):
            body(0, s * NT, 0, True, True, False)
            with eng.Fori(0, (NT - 4) // 2) as p:
                for j in (1, 2):
                    body(2 * p + j, 2 * p + (s * NT + j), j % 2, False, True, False)
            for t in range(NT - 3, NT):
                body(t, s * NT + t, t % 2, False, t + 2 < NT, t == NT - 1)

        @block.sync
        def _(sp):
            sp.dma_start(X0[:, 0:NT - 1, 0:D], x[0:(NT - 1) * P, :].rearrange("(t p) d -> p t d", p=P)).then_inc(x_loaded, 16)
            sp.dma_start(X0[0:LAST, NT - 1, 0:D], x[(NT - 1) * P:N, :]).then_inc(x_loaded, 16)
            sp.dma_start(X0[LAST:P, NT - 1, 0:D], x[0:P - LAST, :]).then_inc(x_loaded, 16)
            for n in range(STEPS):
                sp.dma_start(u_in[:, n, :], U1[n, :, :]).then_inc(w_loaded, 16)
                sp.dma_start(u_in[:, STEPS + n, :], U2[n, :, :]).then_inc(w_loaded, 16)
            sp.dma_start(w_in[:, 0, :], W1[:, :]).then_inc(w_loaded, 16)
            sp.dma_start(w_in[:, 1, :], W3[:, :]).then_inc(w_loaded, 16)
            sp.dma_start(w2_in[:, :], W2[:, :]).then_inc(w_loaded, 16)
            for n, v in enumerate((ln_g, ln_b)):
                sp.dma_start(gb[:, n, :], v.rearrange("(a d) -> a d", a=1).to_broadcast([P, D])).then_inc(w_loaded, 16)
            for s in range(STEPS):
                def load_pair(p, short):
                    for j in range(2):
                        g = 2 * p + (s * NT + j)
                        if not (s == 0 and isinstance(p, int) and p == 0):
                            sp.wait_ge(blk_ready, (g - 2) * (2 * NCH) + NCH)
                        r0 = (2 * p + j) * P
                        if short and j == 1:
                            m = LAST // 16 * 16
                            sp.dma_start(S[0:m, j, 0:N], adj[r0:r0 + m, :]).then_inc(adj_loaded[j], 16)
                            sp.dma_start(S[m:LAST, j, 0:N], adj[r0 + m:N, :]).then_inc(adj_loaded[j], 16)
                        else:
                            sp.dma_start(S[:, j, 0:N], adj[bass.ds(r0, P), :]).then_inc(adj_loaded[j], 16)
                load_pair(0, False)
                with sp.Fori(1, NT // 2 - 1) as p:
                    load_pair(p, False)
                load_pair(NT // 2 - 1, True)
            sp.wait_ge(out_ready, 1)
            sp.dma_start(out[0:(NT - 1) * P, :].rearrange("(t p) d -> p t d", p=P), H[:, 0:NT - 1, :]).then_inc(out_written, 16)
            sp.dma_start(out[(NT - 1) * P:N, :], H[0:LAST, NT - 1, :]).then_inc(out_written, 16)
            sp.wait_ge(out_written, 32)

        @block.gpsimd
        def _(pool):
            pool.memset(ident[:, :], 0.0).then_inc(pool_step, 1)
            pool.wait_ge(pool_step, 1)
            pool.affine_select(out=ident[:, :], in_=ident[:, :], compare_op=ALU.not_equal, fill=1.0,
                               base=0, pattern=[[-1, P]], channel_multiplier=1).then_inc(setup_done, 1)
            pool.memset(X0[:, :, D:D + 1], 1.0).then_inc(setup_done, 1)
            pool.memset(XF[:, :, D:D + 1], 1.0).then_inc(setup_done, 1)
            pool.memset(XA[:, :, D:D + 1], 1.0).then_inc(setup_done, 1)
            pool.memset(S[:, :, N:NP], 0.0).then_inc(setup_done, 1)
            pool.memset(E[:, :, N:NP], 0.0).then_inc(setup_done, 1)
            pool.memset(ones8[:, :], 1.0).then_inc(setup_done, 1)
            pool.memset(flag_in[:, :], 0.0).then_inc(setup_done, 1)
            pool.wait_ge(setup_done, 8)

            for s in range(STEPS):
                def fetch_q(t, g, par):
                    if s or not isinstance(t, int) or t >= 2:
                        pool.wait_ge(logits_ready, (g - 1) * NCH)
                    pool.tensor_copy(q_tile[:, par, :], qT[:, bass.ds(t * P, P)]).then_inc(qt_ready, 1)

                def add_diagonal(t, g, par, last):
                    pool.wait_ge(adj_loaded[par], 8 * g + (8 * (2 - par) + (16 * s if par else 0) + (16 if last else 0)))
                    w = LAST if last else P
                    d = S[:, par, bass.ds(t * P, w)]
                    pool.tensor_tensor(d, d, ident[:, 0:w], ALU.add).then_inc(diag_ready, 1)

                def new_features(g):
                    if not (isinstance(g, int) and g == 0):
                        pool.wait_ge(newT_ready, g)
                        if s == 0:
                            pool.wait_ge(new_saved, g)
                    pool.wait_ge(inv_ready, 2 * (g + 1))
                    pool.tensor_tensor(spare_pool[:, :], ones8[:, 0:1], ones8[:, 0:1], ALU.mult)
                    pool.tensor_scalar(newF[:, :], sumF[:, 0:D], inv[:, 0:1], None, ALU.mult)
                    pool.tensor_scalar(newA[:, :], sumA[:, 0:D], inv[:, 1:2], None, ALU.mult).then_inc(new_ready, 1)

                def save_new(t, g):
                    if s == 0:
                        pool.wait_ge(new_ready, g + 1)
                        pool.tensor_copy(XF[:, bass.ds(t, 1), 0:D], newF[:, :].rearrange("p (a d) -> p a d", a=1))
                        pool.tensor_copy(XA[:, bass.ds(t, 1), 0:D], newA[:, :].rearrange("p (a d) -> p a d", a=1)).then_inc(new_saved, 1)

                def add_out(t, g):
                    base = X0 if s == 0 else H
                    pool.wait_ge(h_copied, g + 1)
                    pool.tensor_tensor(H[:, bass.ds(t, 1), :], h_sb[:, :].rearrange("p (a d) -> p a d", a=1),
                                       base[:, bass.ds(t, 1), 0:D], ALU.add).then_inc(h_added, 1)

                add_diagonal(0, s * NT, 0, False)
                pool.wait_ge(q_done, (s + 1) * NCH)
                fetch_q(0, s * NT, 0)
                fetch_q(1, s * NT + 1, 1)

                def body(t, g, par, first, last):
                    if not last:
                        fetch_q(t + 2, g + 2, par)
                        add_diagonal(t + 1, g + 1, 1 - par, False)
                    if not first:
                        new_features(g - 1)
                        save_new(t - 1, g - 1)
                        add_out(t - 1, g - 1)

                body(0, s * NT, 0, True, False)
                with pool.Fori(0, (NT - 2) // 2 - 1) as p:
                    for j in (1, 2):
                        body(2 * p + j, 2 * p + (s * NT + j), j % 2, False, False)
                for t in range(NT - 3, NT):
                    g = s * NT + t
                    if t + 2 < NT:
                        fetch_q(t + 2, g + 2, t % 2)
                    if t + 1 < NT:
                        add_diagonal(t + 1, g + 1, 1 - t % 2, t + 1 == NT - 1)
                    new_features(g - 1)
                    save_new(t - 1, g - 1)
                    add_out(t - 1, g - 1)
                new_features(s * NT + NT - 1)
                save_new(NT - 1, s * NT + NT - 1)
                add_out(NT - 1, s * NT + NT - 1)

        @block.tensor
        def _(pe):
            pe.wait_ge(setup_done, 1)
            pe.wait_ge(w_loaded, 16 * (2 * STEPS + 5))
            for n in range(2 * STEPS):
                pe.transpose(blk_ps[0][:, n * P:(n + 1) * P], u_in[:, n, :], ident[:, :])
            for n in range(2):
                pe.transpose(blk_ps[1][:, n * DA:(n + 1) * DA], w_in[:, n, :], ident[0:DA, 0:DA])
            pe.transpose(blk_ps[1][0:DA, 2 * DA:3 * DA], w2_in[:, :], ident[0:DA, 0:DA]).then_inc(wT_ready, 1)
            pe.wait_ge(wT_done, 3)
            pe.wait_ge(x_loaded, 48)

            for s in range(STEPS):
                Xf, Xa = (X0, X0) if s == 0 else (XF, XA)
                if s:
                    pe.wait_ge(new_saved, s * NT)
                def turn_features(c):
                    n = s * NCH + c
                    if n >= 2:
                        pe.wait_ge(xT_done, n - 1)
                    for b in range(CW[c] // P):
                        last = pe.transpose(blk_ps[c % 2][:, b * P:(b + 1) * P], Xa[:, c * CH + b, 0:D], ident[:, :])
                    last.then_inc(xT_ready, 1)

                def queries(c):
                    n = s * NCH + c
                    pe.wait_ge(x1_done, n + 1)
                    if n:
                        pe.wait_ge(q_done, n)
                    pe.matmul(newT_ps[0:DA, 0:CW[c]], W2T[:, :], x1T[:, 0:CW[c]], start=True, stop=True).then_inc(q_ready, 1)

                turn_features(0)
                for c in range(NCH):
                    n = s * NCH + c
                    w = CW[c]
                    if c + 1 < NCH:
                        turn_features(c + 1)
                    pe.wait_ge(xT_done, n + 1)
                    if n:
                        pe.wait_ge(k_done, n)
                    pe.matmul(racc[0:DA, 0:w], WT[:, 1, :], xT[:, c % 2, 0:w], start=True, stop=True).then_inc(k_ready, 1)
                    if n:
                        pe.wait_ge(x1_done, n)
                    pe.matmul(aacc[0:DA, 0:w], WT[:, 0, :], xT[:, c % 2, 0:w], start=True, stop=True).then_inc(x1_ready, 1)
                    if c:
                        queries(c - 1)
                queries(NCH - 1)
                pe.wait_ge(k_done, (s + 1) * NCH)
                pe.wait_ge(q_done, (s + 1) * NCH)

                def logits(g, par):
                    pe.wait_ge(qt_ready, g + 1)
                    for c in range(NCH):
                        if not (isinstance(g, int) and g == 0 and c < 2):
                            pe.wait_ge(logits_done, g * NCH + (c - 1))
                        pe.matmul(logit_ps[(c + par) % 2][:, 0:LW[c]], q_tile[:, par, :],
                                  kT[:, c * BANK:c * BANK + LW[c]], start=True, stop=True).then_inc(logits_ready, 1)

                def product(src, rhs, width, acc, base, odd):
                    def turn(c):
                        if not (isinstance(base, int) and base + c < 2):
                            pe.wait_ge(blk_done, base + (c - 1))
                        for b in range(CW[c] // P):
                            j = c * CH + b
                            m = pe.transpose(blk_ps[(c + odd) % 2][:, b * P:(b + 1) * P], src[:, j * P:(j + 1) * P], ident[:, :])
                        m.then_inc(blk_ready, 1)
                    turn(0)
                    for c in range(NCH):
                        if c + 1 < NCH:
                            turn(c + 1)
                        pe.wait_ge(blk_done, base + (c + 1))
                        for b in range(CW[c] // P):
                            j = c * CH + b
                            m = pe.matmul(acc[:, 0:width], blkT[:, (c + odd) % 2, b * P:(b + 1) * P], rhs[:, j, 0:width],
                                          start=(j == 0), stop=(j == NT - 1))
                        m.then_inc(blk_used, 1)

                def tile_out(g):
                    pe.wait_ge(new_ready, g + 1)
                    if not (isinstance(g, int) and g == 0):
                        pe.wait_ge(newT_done, g)
                    pe.transpose(newT_ps[:, 0:P], newF[:, :], ident[:, :])
                    pe.transpose(newT_ps[:, P:2 * P], newA[:, :], ident[:, :]).then_inc(newT_ready, 1)
                    pe.wait_ge(newT_done, g + 1)
                    if not (isinstance(g, int) and g == 0):
                        pe.wait_ge(h_copied, g)
                    pe.matmul(h_ps[:, 0:D], newT[:, 0, :], UT[:, s, :], start=True, stop=False)
                    pe.matmul(h_ps[:, 0:D], newT[:, 1, :], UT[:, STEPS + s, :], start=False, stop=True).then_inc(h_ready, 1)

                logits(s * NT, 0)
                logits(s * NT + 1, 1)

                def body(t, g, par, first, two_more, last):
                    pe.wait_ge(diag_ready, g + 1)
                    if not (isinstance(g, int) and g == 0):
                        pe.wait_ge(sums_ready, g)
                    product(S[:, par, :], Xf, D + 1, racc, g * (2 * NCH), 0)
                    if two_more:
                        logits(g + 2, par)
                    pe.wait_ge(a_ready, g + 1)
                    product(A, Xa, D + 1, aacc, g * (2 * NCH) + NCH, NCH % 2)
                    if not first:
                        tile_out(g - 1)
                over_tiles_ahead(pe, s, body)
                tile_out(s * NT + NT - 1)

        @block.scalar
        def _(act):
            act.wait_ge(wT_ready, 1)
            act.activation(UT[:, :, :], blk_ps[0][:, :].rearrange("p (n d) -> p n d", n=2 * STEPS), ACT.Copy).then_inc(wT_done, 1)
            act.activation(WT[:, :, :], blk_ps[1][:, 0:2 * DA].rearrange("p (n d) -> p n d", n=2), ACT.Copy).then_inc(wT_done, 1)
            act.activation(W2T[:, :], blk_ps[1][0:DA, 2 * DA:3 * DA], ACT.Copy).then_inc(wT_done, 1)
            act.wait_ge(setup_done, 7)
            for s in range(STEPS):
                def empty_features(c):
                    n = s * NCH + c
                    act.wait_ge(xT_ready, n + 1)
                    if n >= 2:
                        act.wait_ge(x1_ready, n - 1)
                    act.activation(xT[:, c % 2, 0:CW[c]], blk_ps[c % 2][:, 0:CW[c]], ACT.Copy).then_inc(xT_done, 1)

                empty_features(0)
                for c in range(NCH):
                    n = s * NCH + c
                    if c + 1 < NCH:
                        empty_features(c + 1)
                    act.wait_ge(x1_ready, n + 1)
                    if n:
                        act.wait_ge(q_ready, n)
                    act.activation(x1T[:, 0:CW[c]], aacc[0:DA, 0:CW[c]], ACT.Copy).then_inc(x1_done, 1)

                def store_logits(g, par):
                    if not (isinstance(g, int) and g < 2):
                        act.wait_ge(a_ready, g - 1)
                    for c in range(NCH):
                        act.wait_ge(logits_ready, g * NCH + (c + 1))
                        act.activation(E[:, par, c * BANK:c * BANK + LW[c]], logit_ps[(c + par) % 2][:, 0:LW[c]],
                                       ACT.Copy).then_inc(logits_done, 1)

                def exponentials(g, par):
                    act.wait_ge(max_ready, g + 1)
                    act.activation(cand[:, par, 0:NC[s]], cand[:, par, 0:NC[s]], ACT.Exp, bias=negm[:, par:par + 1], scale=1.0,
                                   accum_out=csum[:, par:par + 1])
                    act.activation(E[:, par, 0:N], E[:, par, 0:N], ACT.Exp, bias=negm[:, par:par + 1], scale=1.0,
                                   accum_out=Z[:, par:par + 1]).then_inc(e_ready, 1)

                def empty_blocks(base, odd):
                    for c in range(NCH):
                        act.wait_ge(blk_ready, base + (c + 1))
                        if not (isinstance(base, int) and base + c < 2):
                            act.wait_ge(blk_used, base + (c - 1))
                        act.activation(blkT[:, (c + odd) % 2, 0:CW[c]], blk_ps[(c + odd) % 2][:, 0:CW[c]],
                                       ACT.Copy).then_inc(blk_done, 1)

                def empty_new(g):
                    act.wait_ge(newT_ready, g + 1)
                    if not (isinstance(g, int) and g == 0):
                        act.wait_ge(h_ready, g)
                    act.activation(newT[:, :, :], newT_ps[:, 0:2 * P].rearrange("p (n d) -> p n d", n=2),
                                   ACT.Copy).then_inc(newT_done, 1)

                def store_sums(g):
                    if not (isinstance(g, int) and g == 0):
                        act.wait_ge(new_ready, g)
                    act.wait_ge(blk_used, g * (2 * NCH) + NCH)
                    act.activation(sumF[:, :], racc[:, 0:D + 1], ACT.Copy)
                    act.wait_ge(blk_used, (g + 1) * (2 * NCH))
                    act.activation(sumA[:, :], aacc[:, 0:D + 1], ACT.Copy).then_inc(sums_ready, 1)

                def store_out(g):
                    act.wait_ge(h_ready, g + 1)
                    if not (isinstance(g, int) and g == 0):
                        act.wait_ge(h_added, g)
                    act.activation(h_sb[:, :], h_ps[:, 0:D], ACT.Copy).then_inc(h_copied, 1)

                store_logits(s * NT, 0)
                exponentials(s * NT, 0)
                store_logits(s * NT + 1, 1)

                def body(t, g, par, first, two_more, last):
                    if not first:
                        store_sums(g - 1)
                    empty_blocks(g * (2 * NCH), 0)
                    if not last:
                        exponentials(g + 1, 1 - par)
                    if two_more:
                        store_logits(g + 2, par)
                    empty_blocks(g * (2 * NCH) + NCH, NCH % 2)
                    if not first:
                        empty_new(g - 1)
                        store_out(g - 1)
                over_tiles_ahead(act, s, body)
                store_sums(s * NT + NT - 1)
                empty_new(s * NT + NT - 1)
                store_out(s * NT + NT - 1)
            for n in range(2):
                act.wait_ge(var_ready, n + 1)
                act.activation(sd[:, :], sd[:, :], ACT.Sqrt).then_inc(sd_ready, 1)

        @block.vector
        def _(dve):
            v = nc.vector
            class Chain:
                def __init__(self, sem, others=(), skip=0):
                    self.sem, self.n, self.others, self.skip = sem, 0, others, skip
                    dve.sem_clear(sem)

                def post(self, ins):
                    self.n += 1
                    ins.then_inc(self.sem, 1)

                def __call__(self, ins):
                    self.post(ins)
                    if self.others and self.n > self.skip:
                        self.others.pop(0)()
                    dve.wait_ge(self.sem, self.n)

            SKIP = 7

            def col(n, m=1):
                return st[:, n:n + m]

            (DROPZ, THR, LOW, PICK, LOWW, ROOM, TSTAR, GAP, TIE, SLOW, S2, FLOOR, BUDGET, THRLO, THRHI,
             LO, HI, RLO, RHI, WIDTH, FRAC, T2, L2, CSW, TIES, CUT, STEP) = range(27)

            def pick_smallest_kept(link, w, room):
                link(v.tensor_tensor_scan(c8[:, :], ones8[:, :], w8[:, :], 0.0, ALU.mult, ALU.add))
                link(v.tensor_tensor(d8[:, :], c8[:, :], w8[:, :], ALU.subtract))
                link(v.tensor_scalar(d8[:, :], d8[:, :], col(room), BIG, ALU.is_ge, ALU.mult))
                link(v.tensor_tensor(d8[:, :], d8[:, :], w8[:, :], ALU.max))
                link(v.tensor_reduce(col(TSTAR), d8[:, :], AX.X, ALU.min))

            def search(link, c, mass, csum, n_trials, n_looks):
                fact = FACT[:n_trials]
                link(v.scalar_tensor_tensor(out=col(BUDGET), in0=csum, scalar=mass, in1=col(DROPZ),
                                            op0=ALU.subtract, op1=ALU.add))
                link(v.tensor_scalar(col(THR), col(DROPZ), fact[0] / NP, None, ALU.mult))
                for k in range(n_trials):
                    nxt = fact[k + 1] if k + 1 < n_trials else 1.0
                    link(v.scalar_tensor_tensor(out=junkC[:, 0:c.shape[1]], in0=c, scalar=col(THR), in1=c, op0=ALU.is_lt,
                                                op1=ALU.mult, accum_out=col(LOW)))
                    link(v.tensor_scalar(col(PICK), col(LOW), col(BUDGET), nxt - nxt / fact[k], ALU.is_le, ALU.mult))
                    link(v.scalar_tensor_tensor(out=col(THR), in0=col(PICK), scalar=nxt / fact[k], in1=col(THR),
                                                op0=ALU.add, op1=ALU.mult))
                link.post(v.tensor_scalar(col(THRLO), col(THR), 1.0 - SLACK, None, ALU.mult))
                link(v.tensor_scalar(col(THRHI), col(THR), fact[-1] * (1.0 + SLACK), None, ALU.mult))
                link(v.scalar_tensor_tensor(out=junkC[:, 0:c.shape[1]], in0=c, scalar=col(THRHI), in1=c, op0=ALU.is_lt,
                                            op1=ALU.mult, accum_out=col(LOWW)))
                link.post(v.tensor_tensor(col(ROOM), col(LOWW), col(BUDGET), ALU.subtract))
                link.post(v.max(w8[:, :], junkC[:, 0:c.shape[1]]))
                link(v.tensor_reduce(col(FLOOR), c.rearrange("p (n k) -> p n k", k=8)[:, :, 7], AX.X, ALU.max))
                pick_smallest_kept(link, w8, ROOM)
                for look in range(n_looks):
                    if look:
                        link.post(v.tensor_copy(col(PICK), col(TSTAR)))
                        link(v.max(w8[:, :], junkC[:, 0:c.shape[1]]))
                        pick_smallest_kept(link, w8, GAP)
                        link(v.tensor_tensor(col(TSTAR), col(TSTAR), col(PICK), ALU.min))
                    link(v.scalar_tensor_tensor(out=junkC[:, 0:c.shape[1]], in0=c, scalar=col(TSTAR), in1=c, op0=ALU.is_lt,
                                                op1=ALU.mult, accum_out=col(LOW)))
                    link(v.tensor_tensor(col(GAP), col(LOW), col(BUDGET), ALU.subtract))
                link.post(v.tensor_scalar(col(SLOW), col(GAP), 0.0, None, ALU.is_gt))
                link.post(v.tensor_scalar(col(S2), col(TSTAR), 2.0, None, ALU.is_gt))
                link(v.tensor_scalar(col(TIE), col(GAP), col(TSTAR), 0.0, ALU.add, ALU.is_le))
                link(v.tensor_tensor(col(SLOW), col(SLOW), col(S2), ALU.max))
                link(v.tensor_scalar(col(S2), col(TSTAR), col(FLOOR), None, ALU.is_le))
                link(v.tensor_tensor(col(SLOW), col(SLOW), col(S2), ALU.max))
                link(v.scalar_tensor_tensor(out=flag_in[:, 0:1], in0=col(SLOW), scalar=2.0, in1=col(TIE),
                                            op0=ALU.mult, op1=ALU.add))

            def reduce_flag(link):
                link(v.transpose(flag_T[:, :], flag_in[:, :]))
                link(v.tensor_reduce(flag_q[:, :], flag_T[:, :], AX.X, ALU.max))
                for q in range(4):
                    ins = v.tensor_copy(flag_4[0:1, q:q + 1], flag_q[32 * q:32 * q + 1, :])
                    (link if q == 3 else link.post)(ins)
                link(v.tensor_reduce(flag_i[:, :], flag_4[:, :], AX.X, ALU.max))

            def where(link, dst, mask, src):
                link.post(v.copy_predicated(col(dst), mask_i[:, mask:mask + 1], src if not isinstance(src, int) else col(src)))

            def evaluate(link, e, t):
                link(v.scalar_tensor_tensor(out=junk[:, :], in0=e, scalar=col(t), in1=e, op0=ALU.is_lt,
                                            op1=ALU.mult, accum_out=col(L2)))
                link.post(v.tensor_scalar(mask_i[:, 0:1], col(L2), col(DROPZ), None, ALU.is_le))
                link(v.tensor_scalar(mask_i[:, 1:2], col(L2), col(DROPZ), None, ALU.is_gt))

            def settle(link):
                link(v.tensor_scalar(mask_i[:, 0:1], col(SLOW), 0.0, None, ALU.is_equal))
                link(v.tensor_scalar(col(T2), col(TSTAR), 1.0 + 3e-7, None, ALU.mult))
                where(link, LO, 0, TSTAR)
                link(v.copy_predicated(col(HI), mask_i[:, 0:1], col(T2)))

            def mass_below_hi(link, c, mass, csum, out):
                link(v.scalar_tensor_tensor(out=junkC[:, 0:c.shape[1]], in0=c, scalar=col(HI), in1=c, op0=ALU.is_lt,
                                            op1=ALU.mult, accum_out=col(LOW)))
                link(v.tensor_tensor(col(out), col(LOW), csum, ALU.subtract))
                link(v.tensor_tensor(col(out), col(out), mass, ALU.add))

            def first_bracket(link, c, par):
                link.post(v.tensor_copy(col(LO), col(THRLO)))
                link.post(v.tensor_copy(col(RLO), col(DROPZ)))
                link(v.tensor_scalar(col(HI), col(FLOOR), 1.0 + SLACK, col(THRHI), ALU.mult, ALU.max))
                mass_below_hi(link, c, Z[:, par:par + 1], csum[:, par:par + 1], RHI)
                settle(link)

            def next_bracket(link):
                link(v.tensor_tensor(col(THRLO), col(THRLO), col(T2), ALU.min))
                link(v.tensor_tensor(col(LO), col(LO), col(THRLO), ALU.max))
                link(v.tensor_scalar(col(FRAC), col(FLOOR), 1.0 + SLACK, col(THRHI), ALU.mult, ALU.max))
                link(v.tensor_tensor(col(FRAC), col(FRAC), col(T2), ALU.min))
                where(link, HI, 1, FRAC)
                where(link, RLO, 0, L2)
                link(v.tensor_copy(col(WIDTH), col(RHI)))
                mass_below_hi(link, candW[:, :], col(L2), col(CSW), WIDTH)
                link(v.copy_predicated(col(RHI), mask_i[:, 1:2], col(WIDTH)))
                settle(link)

            def level(link, e):
                link(v.tensor_tensor(col(WIDTH), col(HI), col(LO), ALU.subtract))
                link(v.scalar_tensor_tensor(out=col(T2), in0=col(WIDTH), scalar=0.1, in1=col(LO), op0=ALU.mult, op1=ALU.add))
                evaluate(link, e, T2)
                where(link, LO, 0, T2)
                where(link, RLO, 0, L2)
                where(link, HI, 1, T2)
                link(v.copy_predicated(col(RHI), mask_i[:, 1:2], col(L2)))
                link.post(v.tensor_tensor(col(WIDTH), col(HI), col(LO), ALU.subtract))
                link.post(v.scalar_tensor_tensor(out=col(FRAC), in0=col(HI), scalar=-AIM, in1=col(RHI), op0=ALU.mult, op1=ALU.add))
                link(v.tensor_tensor(col(T2), col(RHI), col(RLO), ALU.subtract))
                link(v.tensor_scalar(col(T2), col(T2), 1e-20, None, ALU.max))
                link.post(v.reciprocal(col(T2), col(T2)))
                link(v.tensor_tensor(col(FRAC), col(FRAC), col(DROPZ), ALU.subtract))
                link(v.tensor_tensor(col(FRAC), col(FRAC), col(T2), ALU.mult))
                link(v.tensor_scalar(col(FRAC), col(FRAC), 0.1, 0.9, ALU.max, ALU.min))
                link(v.tensor_tensor(col(FRAC), col(FRAC), col(SLOW), ALU.mult))
                link(v.tensor_tensor(col(WIDTH), col(WIDTH), col(FRAC), ALU.mult))
                link(v.tensor_tensor(col(T2), col(HI), col(WIDTH), ALU.subtract))
                evaluate(link, e, T2)
                for n in range(NT):
                    ins = v.max(candW[:, 8 * n:8 * n + 8], junk[:, n * P:(n + 1) * P])
                    (link if n == NT - 1 else link.post)(ins)
                link(v.tensor_reduce(col(CSW), candW[:, :], AX.X, ALU.add))
                search(link, candW[:, :], col(L2), col(CSW), K_NEXT, W_NEXT)
                reduce_flag(link)

            def full(e):
                link = Chain(s_full)
                link.post(v.memset(col(LO), 0.0))
                link(v.memset(col(STEP), 1.0))
                with dve.Fori(0, K_FULL) as k:
                    link = Chain(s_full)
                    link(v.tensor_tensor(col(THR), col(LO), col(STEP), ALU.add))
                    link(v.scalar_tensor_tensor(out=junk[:, :], in0=e, scalar=col(THR), in1=e, op0=ALU.is_lt,
                                                op1=ALU.mult, accum_out=col(LOW)))
                    link(v.tensor_scalar(col(PICK), col(LOW), col(DROPZ), None, ALU.is_le))
                    link(v.scalar_tensor_tensor(out=col(LO), in0=col(PICK), scalar=col(STEP), in1=col(LO), op0=ALU.mult, op1=ALU.add))
                    link(v.tensor_scalar(col(STEP), col(STEP), 0.5, None, ALU.mult))
                link = Chain(s_full)
                link(v.scalar_tensor_tensor(out=col(THRHI), in0=col(STEP), scalar=4.0, in1=col(LO), op0=ALU.mult, op1=ALU.add))
                link(v.tensor_scalar(col(THRHI), col(THRHI), 1.0 + SLACK, None, ALU.mult))
                link(v.scalar_tensor_tensor(out=junk[:, :], in0=e, scalar=col(THRHI), in1=e, op0=ALU.is_lt,
                                            op1=ALU.mult, accum_out=col(LOWW)))
                link.post(v.tensor_tensor(col(ROOM), col(LOWW), col(DROPZ), ALU.subtract))
                link(v.max(w8[:, :], junk[:, :]))
                pick_smallest_kept(link, w8, ROOM)
                link(v.scalar_tensor_tensor(out=junk[:, :], in0=e, scalar=col(TSTAR), in1=e, op0=ALU.is_lt,
                                            op1=ALU.mult, accum_out=col(LOW)))
                link(v.tensor_tensor(col(GAP), col(LOW), col(DROPZ), ALU.subtract))

            def load_flag():
                return dve.value_load(flag_i[0:1, 0:1], min_val=0, max_val=3)

            for s in range(STEPS):
                def store_queries(c):
                    dve.wait_ge(q_ready, s * NCH + c + 1)
                    v.tensor_copy(qT[:, c * BANK:c * BANK + CW[c]], newT_ps[0:DA, 0:CW[c]]).then_inc(q_done, 1)

                for c in range(NCH):
                    dve.wait_ge(k_ready, s * NCH + c + 1)
                    v.tensor_copy(kT[:, c * BANK:c * BANK + CW[c]], racc[0:DA, 0:CW[c]]).then_inc(k_done, 1)
                    if c:
                        store_queries(c - 1)
                store_queries(NCH - 1)

                def candidates(g, par):
                    def run(n):
                        c, r = n * RUN[s] // BANK, RUN[s]
                        if n * r % BANK == 0:
                            dve.wait_ge(logits_done, g * NCH + (c + 1))
                            v.memset(spare[:, c:c + 1], 0.0)
                        v.max(cand[:, par, 8 * n:8 * n + 8], E[:, par, n * r:min((n + 1) * r, N)]).then_inc(s_max, 1)
                    return [lambda n=n: run(n) for n in range(NP // RUN[s])]

                def maxima(par):
                    dve.wait_ge(s_max, NP // RUN[s])
                    v.tensor_reduce(negm[:, par:par + 1], cand[:, par, 0:NC[s]], AX.X, ALU.max).then_inc(s_max, 1)
                    dve.wait_ge(s_max, NP // RUN[s] + 1)
                    v.tensor_scalar(negm[:, par:par + 1], negm[:, par:par + 1], -1.0, None, ALU.mult).then_inc(max_ready, 1)

                dve.sem_clear(s_max)
                for step in candidates(s * NT, 0):
                    step()
                maxima(0)

                def inverses(link, g, par):
                    if not (isinstance(g, int) and g == 0):
                        dve.wait_ge(new_ready, g)
                    v.memset(spare[:, 0:1], 0.0)
                    dve.wait_ge(sums_ready, g + 1)
                    v.reciprocal(inv[:, 0:1], sumF[:, D:D + 1]).then_inc(inv_ready, 1)
                    link(v.tensor_tensor(den[:, :], sumA[:, D:D + 1], least[:, par:par + 1], ALU.max))
                    v.reciprocal(inv[:, 1:2], den[:, :]).then_inc(inv_ready, 1)

                def body(t, g, par, first, last):
                    e = E[:, par, :]
                    z = Z[:, par:par + 1]
                    others = [] if last else candidates(g + 1, 1 - par)
                    dve.sem_clear(s_max)
                    link = Chain(s_search, others, SKIP)
                    dve.wait_ge(e_ready, g + 1)
                    link(v.tensor_scalar(col(DROPZ), z, DROP, None, ALU.mult))
                    search(link, cand[:, par, 0:NC[s]], z, csum[:, par:par + 1], K_FIRST, W_FIRST)
                    reduce_flag(link)
                    while others:
                        others.pop(0)()
                    if not last:
                        maxima(1 - par)

                    if not first:
                        inverses(link, g - 1, 1 - par)

                    with dve.If(load_flag() > 0):
                        with dve.If(load_flag() > 1):
                            link = Chain(s_level)
                            first_bracket(link, cand[:, par, 0:NC[s]], par)
                            level(link, e)
                            with dve.If(load_flag() > 1):
                                link = Chain(s_level)
                                next_bracket(link)
                                level(link, e)
                                with dve.If(load_flag() > 1):
                                    full(e)
                        link = Chain(s_tie)
                        link.post(v.tensor_scalar(eq[:, :], e, col(TSTAR), None, ALU.is_equal))
                        link(v.reciprocal(col(CUT), col(TSTAR)))
                        link(v.tensor_tensor_scan(junk[:, :], eq[:, :], eq[:, :], 0.0, ALU.add, ALU.max))
                        link(v.scalar_tensor_tensor(out=col(TIES), in0=col(GAP), scalar=col(CUT), in1=junk[:, NP - 1:NP],
                                                    op0=ALU.mult, op1=ALU.add))
                        link(v.tensor_scalar(col(TIES), col(TIES), 0.5, 1.0, ALU.max, ALU.add))
                        link(v.scalar_tensor_tensor(out=eq[:, :], in0=junk[:, :], scalar=col(TIES), in1=eq[:, :],
                                                    op0=ALU.is_ge, op1=ALU.mult))
                        link(v.tensor_scalar(col(CUT), col(TSTAR), -1.0, None, ALU.mult))
                        link(v.scalar_tensor_tensor(out=e, in0=eq[:, :], scalar=col(CUT), in1=e,
                                                    op0=ALU.mult, op1=ALU.add))
                    v.tensor_scalar(least[:, par:par + 1], z, 1e-12, None, ALU.mult)
                    if not (isinstance(g, int) and g == 0):
                        dve.wait_ge(blk_ready, g * (2 * NCH))
                    v.scalar_tensor_tensor(out=A[:, :], in0=e, scalar=col(TSTAR), in1=e, op0=ALU.is_ge,
                                           op1=ALU.mult).then_inc(a_ready, 1)
                over_tiles(dve, s, body)
                inverses(Chain(s_search), s * NT + NT - 1, (NT - 1) % 2)

            link = Chain(s_fin)
            dve.wait_ge(h_added, STEPS * NT)
            dve.wait_ge(w_loaded, 16 * (2 * STEPS + 5))

            def per_row(a):
                return a.rearrange("p (t a) -> p t a", a=1).to_broadcast([P, NT, D])

            sq = junk[:, 0:NT * D].rearrange("p (t d) -> p t d", t=NT)
            for n in range(2):
                link(v.tensor_reduce(mv[:, :], H[:, :, :], AX.X, ALU.add))
                link(v.tensor_scalar(mv[:, :], mv[:, :], 1.0 / D, None, ALU.mult))
                link(v.tensor_tensor(H[:, :, :], H[:, :, :], per_row(mv[:, :]), ALU.subtract))
                link(v.tensor_tensor(sq, H[:, :, :], H[:, :, :], ALU.mult))
                link(v.tensor_reduce(mv[:, :], sq, AX.X, ALU.add))
                v.tensor_scalar(sd[:, :], mv[:, :], 1.0 / D, LN_EPS, ALU.mult, ALU.add).then_inc(var_ready, 1)
                dve.wait_ge(sd_ready, n + 1)
                link(v.reciprocal(rs[:, :], sd[:, :]))
                if n == 0:
                    link(v.tensor_tensor(H[:, :, :], H[:, :, :], per_row(rs[:, :]), ALU.mult))
                    link(v.tensor_tensor(H[:, :, :], H[:, :, :], gb[:, 0:1, :].to_broadcast([P, NT, D]), ALU.mult))
                    link(v.tensor_tensor(H[:, :, :], H[:, :, :], gb[:, 1:2, :].to_broadcast([P, NT, D]), ALU.add))
                    link(v.tensor_tensor(H[:, :, :], H[:, :, :], X0[:, :, 0:D], ALU.add))
                else:
                    v.tensor_tensor(H[:, :, :], H[:, :, :], per_row(rs[:, :]), ALU.mult).then_inc(out_ready, 1)


_INS = ["x", "adj", "L0_gnn_W1", "L0_gnn_W2", "L0_gnn_W3", "L0_gnn_U1", "L0_gnn_U2", "L0_gnn_ln_g", "L0_gnn_ln_b"]


def kernel(**inputs):
    import numpy as _np
    import concourse.bacc as _bacc
    from concourse import mybir as _mybir
    from concourse.bass_utils import run_bass_kernel_spmd as _run

    nc = _bacc.Bacc("TRN2", target_bir_lowering=False, num_devices=1)
    arrays, args = {}, []
    for name in _INS:
        a = _np.ascontiguousarray(inputs[name])
        arrays[f"in_{name}_dram"] = a
        args.append(nc.dram_tensor(f"in_{name}_dram", a.shape, _mybir.dt.from_np(a.dtype), kind="ExternalInput").ap())
    shape, dtype = inputs["x"].shape, _mybir.dt.from_np(_np.dtype("float32"))
    args.append(nc.dram_tensor("out_0_dram", shape, dtype, kind="ExternalOutput").ap())
    gnn_top_p_kernel(nc, *args)
    r = _run(nc, [arrays], core_ids=[0])
    return r.results[0]["out_0_dram"]
```
